# Optimizing a Trainium2 kernel written in Bass

```python
import numpy as np
import jax
import jax.numpy as jnp

def _softmax(x, axis=-1):
    return jax.nn.softmax(x, axis=axis)

def _gelu(x):
    return jax.nn.gelu(x, approximate=True)

def _silu(x):
    return jax.nn.silu(x)

def _sigmoid(x):
    return jax.nn.sigmoid(x)

def _layernorm(x, axis=-1, eps=1e-05):
    m = jnp.mean(x, axis=axis, keepdims=True)
    v = jnp.var(x, axis=axis, keepdims=True)
    return (x - m) / jnp.sqrt(v + eps)

def _scatter_add(tgt, idx, src, axis=0):
    return tgt.at[idx].add(src)

def _segment_sum(src, seg, n):
    return jax.ops.segment_sum(src, seg, n)
kernel_name = 'mk_adj_resnorm_d1_adj_r2_26c6dd'

def setup_inputs(seed: int=0):
    np.random.seed(seed)
    _w = jnp.asarray

    def _rec_inputs():
        import jax
        import jax.numpy as jnp
        _gk = jax.random.key(seed)
        x = -1.394e-06 + 0.9999 * jax.random.normal(jax.random.fold_in(_gk, 1), (64, 128, 256), jnp.float32)
        _a = jax.random.bernoulli(jax.random.fold_in(_gk, 2), 0.03125, (64, 128, 128))
        adj = _a.astype(jnp.int32)
        return (x, adj)
    x, adj = _rec_inputs()

    def _L0_gnn_setup():
        import jax, jax.numpy as jnp
        import numpy as np
        NEG_INF = -1000000000.0
        NEG_SLOPE = 0.2

        def gat_layer(x, mask, W, a_src, a_dst, bias, concat):
            B, N, _ = x.shape
            H, F = a_src.shape
            xl = (x @ W).reshape(B, N, H, F)
            asrc = jnp.einsum('bnhf,hf->bnh', xl, a_src)
            adst = jnp.einsum('bnhf,hf->bnh', xl, a_dst)
            e = jax.nn.leaky_relu(asrc[:, :, None, :] + adst[:, None, :, :], NEG_SLOPE)
            e = jnp.where(mask[..., None], e, NEG_INF)
            attn = jax.nn.softmax(e, axis=1)
            out = jnp.einsum('bsdh,bshf->bdhf', attn, xl)
            if concat:
                out = out.reshape(B, N, H * F)
            else:
                out = out.mean(axis=2)
            return out + bias
        key = jax.random.key(seed)
        ks = jax.random.split(key, 10)
        B, N, Din, Fh, H, Dout = (8, 512, 256, 128, 4, 256)
        s = 0.05
        return {'adj': jax.random.randint(ks[0], (B, N, N), 0, 2, dtype=jnp.int32), 'x': jax.random.normal(ks[1], (B, N, Din), dtype=jnp.float32), 'W1': jax.random.normal(ks[2], (Din, H * Fh), dtype=jnp.float32) * s, 'att_src1': jax.random.normal(ks[3], (H, Fh), dtype=jnp.float32) * s, 'att_dst1': jax.random.normal(ks[4], (H, Fh), dtype=jnp.float32) * s, 'b1': jax.random.normal(ks[5], (H * Fh,), dtype=jnp.float32) * s, 'W2': jax.random.normal(ks[6], (H * Fh, Dout), dtype=jnp.float32) * s, 'att_src2': jax.random.normal(ks[7], (1, Dout), dtype=jnp.float32) * s, 'att_dst2': jax.random.normal(ks[8], (1, Dout), dtype=jnp.float32) * s, 'b2': jax.random.normal(ks[9], (Dout,), dtype=jnp.float32) * s}
    _L0_gnn_all = _L0_gnn_setup()
    _L0_gnn_in = {k: v for k, v in _L0_gnn_all.items() if k in ('W1', 'att_src1', 'att_dst1', 'b1', 'W2', 'att_src2', 'att_dst2', 'b2')}
    del _L0_gnn_all
    return {'x': x, 'adj': adj, 'L0_gnn_W1': _L0_gnn_in['W1'], 'L0_gnn_att_src1': _L0_gnn_in['att_src1'], 'L0_gnn_att_dst1': _L0_gnn_in['att_dst1'], 'L0_gnn_b1': _L0_gnn_in['b1'], 'L0_gnn_W2': _L0_gnn_in['W2'], 'L0_gnn_att_src2': _L0_gnn_in['att_src2'], 'L0_gnn_att_dst2': _L0_gnn_in['att_dst2'], 'L0_gnn_b2': _L0_gnn_in['b2']}

def reference(x, adj, L0_gnn_W1, L0_gnn_att_src1, L0_gnn_att_dst1, L0_gnn_b1, L0_gnn_W2, L0_gnn_att_src2, L0_gnn_att_dst2, L0_gnn_b2):
    import jax
    import jax.numpy as jnp

    def _L0_gnn_ref(adj, x, W1, att_src1, att_dst1, b1, W2, att_src2, att_dst2, b2):
        import jax, jax.numpy as jnp
        import numpy as np
        NEG_INF = -1000000000.0
        NEG_SLOPE = 0.2

        def gat_layer(x, mask, W, a_src, a_dst, bias, concat):
            B, N, _ = x.shape
            H, F = a_src.shape
            xl = (x @ W).reshape(B, N, H, F)
            asrc = jnp.einsum('bnhf,hf->bnh', xl, a_src)
            adst = jnp.einsum('bnhf,hf->bnh', xl, a_dst)
            e = jax.nn.leaky_relu(asrc[:, :, None, :] + adst[:, None, :, :], NEG_SLOPE)
            e = jnp.where(mask[..., None], e, NEG_INF)
            attn = jax.nn.softmax(e, axis=1)
            out = jnp.einsum('bsdh,bshf->bdhf', attn, xl)
            if concat:
                out = out.reshape(B, N, H * F)
            else:
                out = out.mean(axis=2)
            return out + bias
        B, N, _ = adj.shape
        mask = (adj > 0) | jnp.eye(N, dtype=bool)[None]
        h = jax.nn.elu(gat_layer(x, mask, W1, att_src1, att_dst1, b1, concat=True))
        h = gat_layer(h, mask, W2, att_src2, att_dst2, b2, concat=False)
        return h
    x = _layernorm(x + _L0_gnn_ref(adj, x, L0_gnn_W1, L0_gnn_att_src1, L0_gnn_att_dst1, L0_gnn_b1, L0_gnn_W2, L0_gnn_att_src2, L0_gnn_att_dst2, L0_gnn_b2), axis=-1)
    return x

_drawn_inputs = setup_inputs


def setup_inputs(seed=0):
    import zlib

    import numpy as np

    out = dict(_drawn_inputs(seed))
    spreads = {}
    factors = {'L0_gnn_att_dst1': 3.336, 'L0_gnn_att_dst2': 5.181}
    for name, (base, spread) in spreads.items():
        noise = np.random.default_rng([zlib.crc32(name.encode()), seed]).standard_normal(out[name].shape)
        drawn = base * np.exp(spread * noise) if base else spread * noise
        out[name] = jnp.asarray(drawn.astype(out[name].dtype))
    for name, factor in factors.items():
        out[name] = (out[name] * factor).astype(out[name].dtype)
    return out
```

```python
from contextlib import ExitStack

import concourse.bass as bass
from concourse import mybir

P = 128
ALU = mybir.AluOpType
ACT = mybir.ActivationFunctionType
AX = mybir.AxisListType
F32 = mybir.dt.float32
BF16 = mybir.dt.bfloat16
I32 = mybir.dt.int32

NEG_SLOPE = 0.2
LN_EPS = 1e-5
MASKED = -(2.0 ** 100)


def gat_block_program(nc, x, adj, W1, att_src1, att_dst1, b1, W2, att_src2, att_dst2, b2, out):
    B, N, D = x.shape
    H, F = att_src1.shape
    HF = H * F
    DO = W2.shape[1]
    assert N == P and F == P and D % P == 0 and DO == D
    KC = D // P
    HG = 2
    HH = H // HG
    GW = HH * F + 2 * HH
    NS = 2 * H
    SPLIT = 3
    R = SPLIT * NS
    W2C = DO + 2
    XRING = 8
    BODY = XRING
    LAST = 4
    PAIR = 2

    ctx = ExitStack()
    with ctx:
        def sb(name, shape, dt=F32):
            return ctx.enter_context(nc.sbuf_tensor(name, shape, dt))

        def psum(name, shape, dt=F32):
            return ctx.enter_context(nc.psum_tensor(name, shape, dt))

        def sem(name):
            return ctx.enter_context(nc.semaphore(name))

        w1 = sb("w1", [P, KC, HG, GW])
        w2 = sb("w2", [P, H, W2C])
        bias1 = sb("bias1", [P, HG, GW])
        bias2 = sb("bias2", [P, W2C])
        att1 = sb("att1", [P, 2, HF])
        att2 = sb("att2", [P, 2, DO])
        prod1 = sb("prod1", [P, KC, HF])
        prod2 = sb("prod2", [P, H, DO])
        b1_all = sb("b1_all", [P, HF])
        b2_all = sb("b2_all", [P, DO])
        ones = sb("ones", [P, P])
        ident = sb("ident", [P, P])
        ident_bf = sb("ident_bf", [P, P], BF16)
        mask_ident = sb("mask_ident", [P, H, P], BF16)
        edge_limit = sb("edge_limit", [P, P])
        row_sel = sb("row_sel", [R, NS])
        sel_src = sb("sel_src", [R, H, P], BF16)
        sel_dst = sb("sel_dst", [R, H, P], BF16)
        minus_half = sb("minus_half", [P, 1])
        ln_eps = sb("ln_eps", [P, 1])
        zeros = sb("zeros", [P, NS])
        minus_one = sb("minus_one", [P, 1])

        x_sb = sb("x_sb", [P, XRING, D])
        adj_sb = sb("adj_sb", [P, XRING, P], I32)
        no_edge = sb("no_edge", [P, XRING, P], BF16)
        xT = sb("xT", [P, 2, KC, P])
        xl = sb("xl", [P, 4, HG, GW])
        parts = sb("parts", [P, 2, SPLIT, NS], BF16)
        rest = sb("rest", [P, 2, NS])
        score_rows = sb("score_rows", [R, 2, P], BF16)
        score1 = sb("score1", [P, 2, H, P])
        score2 = sb("score2", [P, 2, P])
        lrelu1 = sb("lrelu1", [P, 2, H, P])
        negmax1 = sb("negmax1", [P, 2, H])
        prob1 = sb("prob1", [P, 2, H, P])
        den1 = sb("den1", [P, 2, H])
        rden1 = sb("rden1", [P, 2, H])
        attn1 = sb("attn1", [P, 2, H, P])
        attn1T = sb("attn1T", [P, 2, H, P])
        expu = sb("expu", [P, 2, H, P])
        hT = sb("hT", [P, 2, H, P])
        xl2 = sb("xl2", [P, 2, W2C])
        lrelu2 = sb("lrelu2", [P, 2, P])
        negmax2 = sb("negmax2", [P, 2])
        prob2 = sb("prob2", [P, 2, P])
        den2 = sb("den2", [P, 2])
        rden2 = sb("rden2", [P, 2])
        prob2T = sb("prob2T", [P, 2, P])
        resid = sb("resid", [P, 2, D])
        stats = sb("stats", [P, 2, 6])
        meanvar = sb("meanvar", [P, 2, 2])
        vareps = sb("vareps", [P, 2])
        rstd = sb("rstd", [P, 2])
        y_sb = sb("y_sb", [P, 4, D])

        ps_xT = psum("ps_xT", [P, KC, P])
        ps_xl = psum("ps_xl", [P, HG, 512])
        ps_z1 = psum("ps_z1", [P, H, P])
        ps_pT = psum("ps_pT", [P, H, P])
        ps_u = psum("ps_u", [P, H, P])
        ps_xl2 = psum("ps_xl2", [P, 512])
        ps_l2 = psum("ps_l2", [P, 512])
        ps_rows = ps_xT[0:R, 0, :].bitcast(BF16)[:, 0:P]
        ps_p2T = ps_l2[:, 0:P]
        ps_u2 = ps_l2[:, 0:DO]
        ps_z2 = ps_l2[:, 0:P]

        weights_in = sem("weights_in")
        consts_ready = sem("consts_ready")
        colsum_ready = sem("colsum_ready")
        setup_step = sem("setup_step")
        pool_step = sem("pool_step")
        x_in = [sem(f"x_in{k}") for k in range(XRING // PAIR)]
        adj_in = [sem(f"adj_in{k}") for k in range(XRING // PAIR)]
        y_out = [sem(f"y_out{k}") for k in range(2)]
        xT_made = sem("xT_made")
        xl_made = sem("xl_made")
        rows_made = sem("rows_made")
        z1_made = sem("z1_made")
        pT_made = sem("pT_made")
        u_made = sem("u_made")
        xl2_made = sem("xl2_made")
        z2_made = sem("z2_made")
        p2T_made = sem("p2T_made")
        u2_made = sem("u2_made")
        score1_done = sem("score1_done")
        prob1_done = sem("prob1_done")
        attn1T_done = sem("attn1T_done")
        rows_done = sem("rows_done")
        expu_done = sem("expu_done")
        score2_done = sem("score2_done")
        prob2_done = sem("prob2_done")
        prob2T_done = sem("prob2T_done")
        mask_done = sem("mask_done")
        xT_done = sem("xT_done")
        xl_done = sem("xl_done")
        lrelu1_done = sem("lrelu1_done")
        lrelu2_done = sem("lrelu2_done")
        max1_done = sem("max1_done")
        rden1_done = sem("rden1_done")
        hT_done = sem("hT_done")
        xl2_done = sem("xl2_done")
        max2_done = sem("max2_done")
        rden2_done = sem("rden2_done")
        resid_done = sem("resid_done")
        stats_done = sem("stats_done")
        meanvar_done = sem("meanvar_done")
        y_done = sem("y_done")
        hi_done = sem("hi_done")
        rest_done = sem("rest_done")
        mid_done = sem("mid_done")
        parts_done = sem("parts_done")
        attn1_done = sem("attn1_done")
        vareps_done = sem("vareps_done")
        rstd_done = sem("rstd_done")

        x_pairs = x.rearrange("(q k) n d -> q n k d", k=PAIR)
        adj_pairs = adj.rearrange("(q k) s d -> q s k d", k=PAIR)
        out_pairs = out.rearrange("(q k) n d -> q n k d", k=PAIR)

        STEPS = B + LAST + 1
        LOOP0 = LAST + 5
        LOOPS = (B - PAIR - LOOP0) // BODY
        LOOP1 = LOOP0 + LOOPS * BODY

        def run_steps(eng, step):
            for t in range(LOOP0):
                step(0, t)
            with eng.Fori(0, LOOPS, 1) as i:
                for k in range(LOOP0, LOOP0 + BODY):
                    step(i, k)
            for t in range(LOOP1, STEPS):
                step(0, t)

        def live(t, lag):
            return not isinstance(t, int) or 0 <= t - lag < B

        def begun(t, lag):
            return not isinstance(t, int) or t >= lag

        block = ctx.enter_context(nc.Block())

        @block.sync
        def _(sp):
            def load(q, static_q):
                slot = static_q % (XRING // PAIR)
                a = slot * PAIR
                if static_q * PAIR >= XRING:
                    used = q * PAIR + PAIR - XRING
                    sp.wait_ge(xT_made, used)
                    sp.wait_ge(resid_done, used)
                sp.dma_start(x_sb[:, a:a + PAIR, :], pair_of(x_pairs, q)).then_inc(x_in[slot], 16)
                if static_q * PAIR >= XRING:
                    sp.wait_ge(mask_done, q + 1 - XRING // PAIR)
                sp.dma_start(adj_sb[:, a:a + PAIR, :], pair_of(adj_pairs, q)).then_inc(adj_in[slot], 16)

            def pair_of(ap, q):
                if isinstance(q, int):
                    return ap[q]
                return ap[bass.ds(q, 1)].rearrange("q n k d -> (q n) k d")

            load(0, 0)
            for c in range(KC):
                sp.dma_start(w1[:, c, :, 0:HH * F],
                             W1[c * P:(c + 1) * P, :].rearrange("p (j n) -> p j n", j=HG)).then_inc(weights_in, 16)

            def step(i, k):
                t = BODY * i + k
                if k % PAIR == 0 and live(t, -PAIR):
                    load(BODY // PAIR * i + k // PAIR + 1, k // PAIR + 1)
                lag = LAST + 2
                if (k - lag) % PAIR == PAIR - 1 and live(t, lag):
                    q = BODY // PAIR * i + (k - lag) // PAIR
                    slot = (k - lag) // PAIR % 2
                    sp.wait_ge(y_done, t - lag + 1)
                    sp.dma_start(pair_of(out_pairs, q), y_sb[:, slot * PAIR:slot * PAIR + PAIR, :]).then_inc(y_out[slot], 16)

            run_steps(sp, step)
            step(0, STEPS)
            for s in y_out:
                sp.wait_ge(s, 16 * (B // PAIR // 2))

        @block.gpsimd
        def _(pool):
            nc.gpsimd.memset(ones[:], 1.0).then_inc(pool_step, 1)
            nc.gpsimd.memset(edge_limit[:], 0.0).then_inc(pool_step, 1)
            nc.gpsimd.memset(bias1[:], 0.0).then_inc(pool_step, 1)
            nc.gpsimd.memset(minus_half[:], -0.5).then_inc(pool_step, 1)
            nc.gpsimd.memset(minus_one[:], -1.0).then_inc(pool_step, 1)
            nc.gpsimd.memset(ln_eps[:], LN_EPS).then_inc(pool_step, 1)
            nc.gpsimd.memset(zeros[:], 0.0).then_inc(pool_step, 1)
            pool.wait_ge(pool_step, 7)
            nc.gpsimd.affine_select(out=ident[:], in_=ones[:], compare_op=ALU.is_equal, fill=0.0, base=0,
                                    pattern=[[-1, P]], channel_multiplier=1).then_inc(pool_step, 1)
            nc.gpsimd.affine_select(out=edge_limit[:], in_=edge_limit[:], compare_op=ALU.not_equal, fill=-3e38, base=0,
                                    pattern=[[-1, P]], channel_multiplier=1).then_inc(pool_step, 1)

            def step(i, k):
                t = BODY * i + k
                if live(t, 0):
                    src = xl[:, k % 4, :, HH * F:GW]
                    b = k % 2
                    hi, mid, lo = (parts[:, b, p, :].rearrange("p (j c) -> p j c", j=HG) for p in range(SPLIT))
                    no_shift = zeros[:].rearrange("p (j c) -> p j c", j=HG)
                    rst = rest[:, b, :].rearrange("p (j c) -> p j c", j=HG)
                    pool.wait_ge(xl_done, t + 1)
                    if begun(t, 2):
                        pool.wait_ge(rows_made, t - 1)
                    nc.gpsimd.tensor_tensor(hi, src, no_shift, ALU.add).then_inc(hi_done, 1)
                    pool.wait_ge(hi_done, t + 1)
                    nc.gpsimd.tensor_tensor(rst, src, hi, ALU.subtract).then_inc(rest_done, 1)
                    pool.wait_ge(rest_done, t + 1)
                    nc.gpsimd.tensor_tensor(mid, rst, no_shift, ALU.add).then_inc(mid_done, 1)
                    pool.wait_ge(mid_done, t + 1)
                    nc.gpsimd.tensor_tensor(lo, rst, mid, ALU.subtract).then_inc(parts_done, 1)
                if live(t, 1):
                    b = (k - 1) % 2
                    pool.wait_ge(rden1_done, t)
                    if begun(t, 3):
                        pool.wait_ge(pT_made, t - 2)
                    nc.gpsimd.tensor_tensor(attn1[:, b], prob1[:, b],
                                            rden1[:, b, :].unsqueeze(2).broadcast_to([P, H, P]),
                                            ALU.mult).then_inc(attn1_done, 1)
                if live(t, 5):
                    b = (k - 5) % 2
                    pool.wait_ge(meanvar_done, t - 4)
                    nc.gpsimd.tensor_tensor(vareps[:, b:b + 1], meanvar[:, b, 1:2], ln_eps[:], ALU.add).then_inc(vareps_done, 1)
                    pool.wait_ge(vareps_done, t - 4)
                    if begun(t, 7):
                        pool.wait_ge(y_done, t - 6)
                    nc.gpsimd.tensor_tensor(rstd[:, b:b + 1], vareps[:, b:b + 1], minus_half[:],
                                            ALU.pow).then_inc(rstd_done, 1)

            run_steps(pool, step)

        @block.scalar
        def _(act):
            act.dma_start(att1[:, 0, :], att_src1.rearrange("h f -> (h f)").partition_broadcast(P)).then_inc(weights_in, 16)
            act.dma_start(att1[:, 1, :], att_dst1.rearrange("h f -> (h f)").partition_broadcast(P)).then_inc(weights_in, 16)
            act.dma_start(b1_all[:], b1.partition_broadcast(P)).then_inc(weights_in, 16)
            act.dma_start(w2[:, :, 0:DO], W2.rearrange("(h p) n -> p h n", p=P)).then_inc(weights_in, 16)
            act.dma_start(att2[:, 0, :], att_src2.rearrange("h f -> (h f)").partition_broadcast(P)).then_inc(weights_in, 16)
            act.dma_start(att2[:, 1, :], att_dst2.rearrange("h f -> (h f)").partition_broadcast(P)).then_inc(weights_in, 16)
            act.dma_start(b2_all[:], b2.partition_broadcast(P)).then_inc(weights_in, 16)
            act.wait_ge(pool_step, 7)

            def step(i, k):
                t = BODY * i + k
                if live(t, 3):
                    b = (k - 3) % 2
                    act.wait_ge(u_made, t - 2)
                    if begun(t, 5):
                        act.wait_ge(hT_done, t - 4)
                    nc.scalar.activation(expu[:, b], ps_u[:, :, :], ACT.Exp, bias=minus_one[:, 0:1]).then_inc(expu_done, 1)
                if live(t, 4):
                    b = (k - 4) % 2
                    act.wait_ge(z2_made, t - 3)
                    if begun(t, 6):
                        act.wait_ge(lrelu2_done, t - 5)
                    nc.scalar.activation(score2[:, b], ps_z2, ACT.Identity, bias=xl2[:, b, DO + 1:DO + 2]).then_inc(score2_done, 1)
                if live(t, 1):
                    b = (k - 1) % 2
                    act.wait_ge(z1_made, t)
                    if begun(t, 3):
                        act.wait_ge(lrelu1_done, t - 2)
                    nc.scalar.copy(score1[:, b], ps_z1[:, :, :]).then_inc(score1_done, 1)
                if live(t, 4):
                    b = (k - 4) % 2
                    act.wait_ge(max2_done, t - 3)
                    if begun(t, 6):
                        act.wait_ge(p2T_made, t - 5)
                    if begun(t, 6):
                        act.wait_ge(rden2_done, t - 5)
                    nc.scalar.activation(prob2[:, b], lrelu2[:, b], ACT.Exp, bias=negmax2[:, b:b + 1],
                                         accum_out=den2[:, b:b + 1]).then_inc(prob2_done, 1)
                if live(t, 1):
                    b = (k - 1) % 2
                    act.wait_ge(max1_done, t)
                    if begun(t, 3):
                        act.wait_ge(attn1_done, t - 2)
                    for h in range(H):
                        last = nc.scalar.activation(prob1[:, b, h], lrelu1[:, b, h], ACT.Exp, bias=negmax1[:, b, h:h + 1],
                                                    accum_out=den1[:, b, h:h + 1])
                    last.then_inc(prob1_done, 1)
                if live(t, 4):
                    b = (k - 4) % 2
                    act.wait_ge(p2T_made, t - 3)
                    if begun(t, 6):
                        act.wait_ge(u2_made, t - 5)
                    nc.scalar.copy(prob2T[:, b], ps_p2T).then_inc(prob2T_done, 1)
                if live(t, 2):
                    b = (k - 2) % 2
                    act.wait_ge(pT_made, t - 1)
                    if begun(t, 4):
                        act.wait_ge(u_made, t - 3)
                    nc.scalar.copy(attn1T[:, b], ps_pT[:, :, :]).then_inc(attn1T_done, 1)
                if live(t, 0):
                    b = k % 2
                    act.wait_ge(rows_made, t + 1)
                    if begun(t, 2):
                        act.wait_ge(z1_made, t - 1)
                    nc.scalar.copy(score_rows[:, b], ps_rows).then_inc(rows_done, 1)

            run_steps(act, step)

        @block.vector
        def _(dve):
            done = [0]

            def settle(last):
                done[0] += 1
                last.then_inc(setup_step, 1)
                dve.wait_ge(setup_step, done[0])

            dve.wait_ge(pool_step, 9)
            nc.vector.tensor_copy(ident_bf[:], ident[:])
            nc.vector.tensor_scalar(mask_ident[:], ident[:].unsqueeze(1).broadcast_to([P, H, P]), MASKED, None, ALU.mult)
            settle(nc.vector.tensor_reduce(row_sel[:], ident[0:R, 0:R].rearrange("r (p c) -> r c p", c=NS), AX.X, ALU.add))
            chosen = row_sel[:].rearrange("r (j s h) -> r j s h", j=HG, s=2)
            for s, sel in ((0, sel_src), (1, sel_dst)):
                for j in range(HG):
                    nc.vector.tensor_copy(sel[:, j * HH:(j + 1) * HH, :], chosen[:, j, s, :].unsqueeze(2).broadcast_to([R, HH, P]))
            dve.wait_ge(weights_in, 16 * 9)
            for s in range(2):
                settle(score_product(nc, prod1, w1, att1, s, KC, HG, HH * F))
                for c in range(KC):
                    last = nc.vector.tensor_reduce(w1[:, c, :, HH * F + s * HH:HH * F + (s + 1) * HH],
                                                   prod1[:, c, :].rearrange("p (j h f) -> p j h f", j=HG, f=F), AX.X, ALU.add)
                settle(last)
                settle(nc.vector.tensor_tensor(prod2[:], w2[:, :, 0:DO], att2[:, s, :].unsqueeze(1).broadcast_to([P, H, DO]), ALU.mult))
                settle(nc.vector.tensor_reduce(w2[:, :, DO + s:DO + s + 1], prod2[:], AX.X, ALU.add))
            nc.vector.tensor_scalar(bias1[:, :, 0:HH * F], b1_all[:].rearrange("p (j n) -> p j n", j=HG), 1.0, None, ALU.add)\
                .then_inc(consts_ready, 1)
            dve.wait_ge(colsum_ready, 1)
            nc.vector.tensor_tensor(bias2[:, 0:DO], b2_all[:], ps_xl2[:, 0:DO], ALU.subtract)
            settle(nc.vector.tensor_scalar(bias2[:, DO:W2C], ps_xl2[:, DO:W2C], -1.0, None, ALU.mult))

            def step(i, k):
                t = BODY * i + k
                if k % PAIR == 0 and live(t, 0):
                    s = k % XRING
                    slot = k // PAIR % (XRING // PAIR)
                    dve.wait_ge(adj_in[slot], 16 * (i + k // XRING + 1))
                    if begun(t, XRING - PAIR + 1):
                        dve.wait_ge(z2_made, t + PAIR - XRING)
                    nc.vector.tensor_tensor(no_edge[:, s:s + PAIR, :], adj_sb[:, s:s + PAIR, :],
                                            edge_limit[:].unsqueeze(1).broadcast_to([P, PAIR, P]), ALU.is_le).then_inc(mask_done, 1)
                if live(t, 5):
                    dve.wait_ge(stats_done, t - 4)
                if live(t, 0):
                    dve.wait_ge(xT_made, t + 1)
                    if begun(t, 2):
                        dve.wait_ge(xl_made, t - 1)
                    nc.vector.tensor_copy(xT[:, k % 2], ps_xT[:, :, :]).then_inc(xT_done, 1)
                if live(t, 5):
                    b = (k - 5) % 2
                    nc.vector.bn_aggr(meanvar[:, b], stats[:, b]).then_inc(meanvar_done, 1)
                if live(t, 3):
                    b = (k - 3) % 2
                    dve.wait_ge(expu_done, t - 2)
                    if begun(t, 5):
                        dve.wait_ge(xl2_made, t - 4)
                    nc.vector.scalar_tensor_tensor(hT[:, b], expu[:, b], 1.0, ps_u[:, :, :], ALU.min, ALU.max).then_inc(hT_done, 1)
                if live(t, 4):
                    b = (k - 4) % 2
                    dve.wait_ge(score2_done, t - 3)
                    if begun(t, 6):
                        dve.wait_ge(prob2_done, t - 5)
                    nc.vector.scalar_tensor_tensor(lrelu2[:, b], score2[:, b], NEG_SLOPE, score2[:, b], ALU.mult,
                                                   ALU.max).then_inc(lrelu2_done, 1)
                    dve.wait_ge(lrelu2_done, t - 3)
                    nc.vector.tensor_reduce(negmax2[:, b:b + 1], lrelu2[:, b], AX.X, ALU.max, negate=True).then_inc(max2_done, 1)
                if live(t, 1):
                    b = (k - 1) % 2
                    dve.wait_ge(score1_done, t)
                    if begun(t, 3):
                        dve.wait_ge(prob1_done, t - 2)
                    nc.vector.scalar_tensor_tensor(lrelu1[:, b], score1[:, b], NEG_SLOPE, score1[:, b], ALU.mult,
                                                   ALU.max).then_inc(lrelu1_done, 1)
                    dve.wait_ge(lrelu1_done, t)
                    nc.vector.tensor_reduce(negmax1[:, b], lrelu1[:, b], AX.X, ALU.max, negate=True).then_inc(max1_done, 1)
                if live(t, 0):
                    dve.wait_ge(xl_made, t + 1)
                    if begun(t, 4):
                        dve.wait_ge(u_made, t - 3)
                    nc.vector.tensor_tensor(xl[:, k % 4], ps_xl[:, :, 0:GW], bias1[:], ALU.add).then_inc(xl_done, 1)
                if live(t, 4):
                    b = (k - 4) % 2
                    dve.wait_ge(prob2_done, t - 3)
                    if begun(t, 6):
                        dve.wait_ge(resid_done, t - 5)
                    nc.vector.reciprocal(rden2[:, b:b + 1], den2[:, b:b + 1]).then_inc(rden2_done, 1)
                if live(t, 1):
                    b = (k - 1) % 2
                    dve.wait_ge(prob1_done, t)
                    if begun(t, 3):
                        dve.wait_ge(attn1_done, t - 2)
                    nc.vector.reciprocal(rden1[:, b], den1[:, b]).then_inc(rden1_done, 1)
                if live(t, 3):
                    b = (k - 3) % 2
                    dve.wait_ge(xl2_made, t - 2)
                    if begun(t, 5):
                        dve.wait_ge(u2_made, t - 4)
                    nc.vector.tensor_tensor(xl2[:, b], ps_xl2[:, 0:W2C], bias2[:], ALU.add).then_inc(xl2_done, 1)
                if live(t, 4):
                    b = (k - 4) % 2
                    dve.wait_ge(u2_made, t - 3)
                    dve.wait_ge(rden2_done, t - 3)
                    if begun(t, 6):
                        dve.wait_ge(y_done, t - 5)
                    nc.vector.scalar_tensor_tensor(resid[:, b], ps_u2, rden2[:, b:b + 1], x_sb[:, (k - 4) % XRING],
                                                   ALU.mult, ALU.add).then_inc(resid_done, 1)
                    dve.wait_ge(resid_done, t - 3)
                    nc.vector.bn_stats(stats[:, b], resid[:, b]).then_inc(stats_done, 1)
                if live(t, 5):
                    b, slot = (k - 5) % 2, (k - 5) % 4
                    dve.wait_ge(rstd_done, t - 4)
                    if begun(t, 9):
                        dve.wait_ge(y_out[slot // PAIR], 16 * (BODY // 4 * i + (k - 5) // 4))
                    nc.vector.tensor_scalar(y_sb[:, slot, :], resid[:, b, :], meanvar[:, b, 0:1], rstd[:, b:b + 1],
                                            ALU.subtract, ALU.mult).then_inc(y_done, 1)

            run_steps(dve, step)

        @block.tensor
        def _(pe):
            def transpose_x(i, k):
                t = BODY * i + k
                slot = k // PAIR % (XRING // PAIR)
                pe.wait_ge(x_in[slot], 16 * (i + k // XRING + 1))
                if begun(t, 1):
                    pe.wait_ge(xT_done, t)
                if begun(t, 1):
                    pe.wait_ge(rows_done, t)
                for c in range(KC):
                    last = nc.tensor.transpose(ps_xT[:, c, :], x_sb[:, k % XRING, c * P:(c + 1) * P], ident[:])
                last.then_inc(xT_made, 1)

            def step(i, k):
                t = BODY * i + k
                if live(t, 0):
                    pe.wait_ge(xT_done, t + 1)
                    if begun(t, 1):
                        pe.wait_ge(xl_done, t)
                    for j in range(HG):
                        for c in range(KC):
                            last = nc.tensor.matmul(ps_xl[:, j, 0:GW], xT[:, k % 2, c, :], w1[:, c, j, :],
                                                    start=(c == 0), stop=(c == KC - 1))
                    last.then_inc(xl_made, 1)
                if live(t, 4):
                    b = (k - 4) % 2
                    pe.wait_ge(prob2_done, t - 3)
                    nc.tensor.transpose(ps_p2T, prob2[:, b], ident[:]).then_inc(p2T_made, 1)
                if live(t, 2):
                    b = (k - 2) % 2
                    pe.wait_ge(attn1_done, t - 1)
                    if begun(t, 3):
                        pe.wait_ge(attn1T_done, t - 2)
                    for h in range(H):
                        last = nc.tensor.transpose(ps_pT[:, h, :], attn1[:, b, h], ident[:])
                    last.then_inc(pT_made, 1)
                if live(t, 3):
                    b = (k - 3) % 2
                    pe.wait_ge(hT_done, t - 2)
                    if begun(t, 4):
                        pe.wait_ge(xl2_done, t - 3)
                    for h in range(H):
                        last = nc.tensor.matmul(ps_xl2[:, 0:W2C], hT[:, b, h], w2[:, h, :], start=(h == 0), stop=(h == H - 1))
                    last.then_inc(xl2_made, 1)
                if live(t, 4):
                    b = (k - 4) % 2
                    pe.wait_ge(prob2T_done, t - 3)
                    nc.tensor.matmul(ps_u2, prob2T[:, b], xl2[:, b, 0:DO], start=True, stop=True).then_inc(u2_made, 1)
                if live(t, 0):
                    pe.wait_ge(parts_done, t + 1)
                    nc.tensor.transpose(ps_rows, parts[:, k % 2].rearrange("p a b -> p (a b)"), ident_bf[:]).then_inc(rows_made, 1)
                if live(t, 2):
                    b = (k - 2) % 2
                    pe.wait_ge(attn1T_done, t - 1)
                    if begun(t, 3):
                        pe.wait_ge(hT_done, t - 2)
                    for h in range(H):
                        j, hh = h // HH, h % HH
                        last = nc.tensor.matmul(ps_u[:, h, :], xl[:, (k - 2) % 4, j, hh * F:(hh + 1) * F], attn1T[:, b, h],
                                                start=True, stop=True)
                    last.then_inc(u_made, 1)
                if live(t, -1):
                    transpose_x(i, k + 1)
                if live(t, 3):
                    b = (k - 3) % 2
                    pe.wait_ge(xl2_done, t - 2)
                    if begun(t, 4):
                        pe.wait_ge(resid_done, t - 3)
                    nc.tensor.matmul(ps_z2, no_edge[:, (k - 3) % XRING], mask_ident[:, 0, :], start=True, stop=False)
                    nc.tensor.matmul(ps_z2, xl2[:, b, DO:DO + 1].broadcast_to([P, P]), ident[:],
                                     start=False, stop=True).then_inc(z2_made, 1)
                if live(t, 0):
                    b = k % 2
                    pe.wait_ge(mask_done, BODY // PAIR * i + k // PAIR + 1)
                    pe.wait_ge(rows_done, t + 1)
                    if begun(t, 1):
                        pe.wait_ge(score1_done, t)
                    z = ps_z1[:].rearrange("p h d -> p (h d)")
                    nc.tensor.matmul(z, no_edge[:, k % XRING], mask_ident[:].rearrange("p h d -> p (h d)"), start=True, stop=False)
                    nc.tensor.matmul(z, score_rows[:, b], sel_dst[:].rearrange("p h d -> p (h d)"), start=False, stop=False)
                    for h in range(H):
                        last = nc.tensor.matmul(ps_z1[:, h, :], sel_src[:, h], score_rows[:, b], start=False, stop=(h == H - 1))
                    last.then_inc(z1_made, 1)

            pe.wait_ge(pool_step, 9)
            pe.wait_ge(consts_ready, 1)
            for h in range(H):
                last = nc.tensor.matmul(ps_xl2[:, 0:W2C], ones[:], w2[:, h, :], start=(h == 0), stop=(h == H - 1))
            last.then_inc(colsum_ready, 1)
            transpose_x(0, 0)
            run_steps(pe, step)


def score_product(nc, prod, w, att, s, chunks, groups, width):
    for c in range(chunks):
        last = nc.vector.tensor_tensor(prod[:, c, :].rearrange("p (j n) -> p j n", j=groups), w[:, c, :, 0:width],
                                       att[:, s, :].rearrange("p (j n) -> p j n", j=groups), ALU.mult)
    return last


_INS = ['x', 'adj', 'L0_gnn_W1', 'L0_gnn_att_src1', 'L0_gnn_att_dst1', 'L0_gnn_b1', 'L0_gnn_W2', 'L0_gnn_att_src2',
        'L0_gnn_att_dst2', 'L0_gnn_b2']


def kernel(**inputs):
    import numpy as _np
    import concourse.bacc as _bacc
    from concourse import mybir as _mybir
    from concourse.bass_utils import run_bass_kernel_spmd as _run

    nc = _bacc.Bacc("TRN2", target_bir_lowering=False, num_devices=1)
    arrays, args = {}, []
    for name in _INS:
        a = _np.ascontiguousarray(inputs[name])
        arrays[f"in_{name}_dram"] = a
        args.append(nc.dram_tensor(f"in_{name}_dram", a.shape, _mybir.dt.from_np(a.dtype), kind="ExternalInput").ap())
    shape = tuple(inputs['x'].shape)
    args.append(nc.dram_tensor("out_0_dram", shape, _mybir.dt.float32, kind="ExternalOutput").ap())
    gat_block_program(nc, *args)
    r = _run(nc, [arrays], core_ids=[0])
    return r.results[0]["out_0_dram"]
```

```python
from contextlib import ExitStack

import concourse.bass as bass
from concourse import mybir

P = 128
ALU = mybir.AluOpType
ACT = mybir.ActivationFunctionType
AX = mybir.AxisListType
F32 = mybir.dt.float32
F32R = mybir.dt.float32r
BF16 = mybir.dt.bfloat16
I32 = mybir.dt.int32

NEG_SLOPE = 0.2
LN_EPS = 1e-5
MASKED = -(2.0 ** 100)


def gat_block_program(nc, x, xT, adj, W1, att_src1, att_dst1, b1, W2, att_src2, att_dst2, b2, out):
    PAIRS, N, PAIR, D = x.shape
    B = PAIRS * PAIR
    H, F = att_src1.shape
    HF = H * F
    DO = W2.shape[1]
    assert N == P and F == P and D % P == 0 and DO == D
    KC = D // P
    HG = 2
    HH = H // HG
    GW = HH * F + 2 * HH
    NS = 2 * H
    SPLIT = 3
    R = SPLIT * NS
    W2C = DO + 2
    RING = 8
    BODY = RING
    LAST = 6

    ctx = ExitStack()
    with ctx:
        def sb(name, shape, dt=F32):
            return ctx.enter_context(nc.sbuf_tensor(name, shape, dt))

        def psum(name, shape, dt=F32):
            return ctx.enter_context(nc.psum_tensor(name, shape, dt))

        def sem(name):
            return ctx.enter_context(nc.semaphore(name))

        w1 = sb("w1", [P, KC, HG, GW])
        w1_hi = sb("w1_hi", [P, KC, HG, GW], F32R)
        w1_lo = sb("w1_lo", [P, KC, HG, GW], F32R)
        w2 = sb("w2", [P, H, W2C])
        w2_hi = sb("w2_hi", [P, H, W2C], F32R)
        w2_lo = sb("w2_lo", [P, H, W2C], F32R)
        bias1 = sb("bias1", [P, HG, GW])
        bias2 = sb("bias2", [P, W2C])
        att1 = sb("att1", [P, 2, HG, HH * F])
        att2 = sb("att2", [P, 2, DO])
        prod1 = sb("prod1", [P, 2, KC, HG, HH * F])
        prod2 = sb("prod2", [P, 2, H, DO])
        b1_all = sb("b1_all", [P, HF])
        b2_all = sb("b2_all", [P, DO])
        ones = sb("ones", [P, P])
        ident = sb("ident", [P, P])
        ident_bf = sb("ident_bf", [P, P], BF16)
        mask_ident = sb("mask_ident", [P, H, P], BF16)
        edge_limit = sb("edge_limit", [P, P])
        row_sel = sb("row_sel", [R, NS])
        sel_src = sb("sel_src", [R, H, P], BF16)
        sel_dst = sb("sel_dst", [R, H, P], BF16)
        minus_half = sb("minus_half", [P, 1])
        ln_eps = sb("ln_eps", [P, 1])
        zeros = sb("zeros", [P, NS])
        minus_one = sb("minus_one", [P, 1])

        x_sb = sb("x_sb", [P, RING, D])
        xT_sb = sb("xT_sb", [P, RING, KC, P])
        adj_sb = sb("adj_sb", [P, RING, P], I32)
        no_edge = sb("no_edge", [P, RING, P], BF16)
        xT_hi = sb("xT_hi", [P, 2, KC, P], F32R)
        xT_lo = sb("xT_lo", [P, 2, KC, P], F32R)
        xl = sb("xl", [P, 4, HG, GW])
        parts = sb("parts", [P, 2, SPLIT, NS], BF16)
        rest = sb("rest", [P, 2, NS])
        score_rows = sb("score_rows", [R, 2, P], BF16)
        score1 = sb("score1", [P, 2, H, P])
        lrelu1 = sb("lrelu1", [P, 2, H, P])
        negmax1 = sb("negmax1", [P, 2, H])
        prob1 = sb("prob1", [P, 2, H, P])
        den1 = sb("den1", [P, 2, H])
        rden1 = sb("rden1", [P, 2, H])
        attn1 = sb("attn1", [P, 2, H, P])
        attn1T = sb("attn1T", [P, 2, H, P])
        expu = sb("expu", [P, 2, H, P])
        hT = sb("hT", [P, 2, H, P])
        hT_hi = sb("hT_hi", [P, 2, H, P], F32R)
        hT_lo = sb("hT_lo", [P, 2, H, P], F32R)
        xl2 = sb("xl2", [P, 2, W2C])
        score2 = sb("score2", [P, 2, P])
        lrelu2 = sb("lrelu2", [P, 2, P])
        negmax2 = sb("negmax2", [P, 2])
        prob2 = sb("prob2", [P, 2, P])
        den2 = sb("den2", [P, 2])
        rden2 = sb("rden2", [P, 2])
        prob2T = sb("prob2T", [P, 2, P])
        resid = sb("resid", [P, 2, D])
        stats = sb("stats", [P, 2, 6])
        meanvar = sb("meanvar", [P, 2, 2])
        vareps = sb("vareps", [P, 2])
        rstd = sb("rstd", [P, 2])
        y_sb = sb("y_sb", [P, 4, D])

        ps_small = psum("ps_small", [P, 512])
        ps_xl = psum("ps_xl", [P, HG, 512])
        ps_z1 = psum("ps_z1", [P, H, P])
        ps_pT = psum("ps_pT", [P, H, P])
        ps_u = psum("ps_u", [P, H, P])
        ps_xl2 = psum("ps_xl2", [P, 512])
        ps_l2 = psum("ps_l2", [P, 512])
        ps_z2 = ps_small[:, 0:P]
        ps_rows = ps_small[0:R, 0:P].bitcast(BF16)[:, 0:P]
        ps_p2T = ps_l2[:, 0:P]
        ps_u2 = ps_l2[:, 0:DO]

        w1_in = sem("w1_in")
        w2_in = sem("w2_in")
        consts_ready = sem("consts_ready")
        prod1_ready = sem("prod1_ready")
        prod2_ready = sem("prod2_ready")
        w1_ready = sem("w1_ready")
        w2_ready = sem("w2_ready")
        bias2_ready = sem("bias2_ready")
        colsum_ready = sem("colsum_ready")
        setup_step = sem("setup_step")
        x_in = [sem(f"x_in{k}") for k in range(RING // PAIR)]
        xT_in = [sem(f"xT_in{k}") for k in range(RING // PAIR)]
        adj_in = [sem(f"adj_in{k}") for k in range(RING // PAIR)]
        y_out = [sem(f"y_out{k}") for k in range(2)]
        xl_made = sem("xl_made")
        rows_made = sem("rows_made")
        z1_made = sem("z1_made")
        pT_made = sem("pT_made")
        u_made = sem("u_made")
        xl2_made = sem("xl2_made")
        z2_made = sem("z2_made")
        p2T_made = sem("p2T_made")
        u2_made = sem("u2_made")
        score1_done = sem("score1_done")
        prob1_done = sem("prob1_done")
        attn1T_done = sem("attn1T_done")
        rows_done = sem("rows_done")
        expu_done = sem("expu_done")
        h_hi_done = sem("h_hi_done")
        score2_done = sem("score2_done")
        prob2_done = sem("prob2_done")
        prob2T_done = sem("prob2T_done")
        mask_done = sem("mask_done")
        x_hi_done = sem("x_hi_done")
        xl_done = sem("xl_done")
        lrelu1_done = sem("lrelu1_done")
        lrelu2_done = sem("lrelu2_done")
        max1_done = sem("max1_done")
        rden1_done = sem("rden1_done")
        hT_done = sem("hT_done")
        xl2_done = sem("xl2_done")
        max2_done = sem("max2_done")
        rden2_done = sem("rden2_done")
        resid_done = sem("resid_done")
        stats_done = sem("stats_done")
        meanvar_done = sem("meanvar_done")
        y_done = sem("y_done")
        hi_done = sem("hi_done")
        rest_done = sem("rest_done")
        mid_done = sem("mid_done")
        parts_done = sem("parts_done")
        attn1_done = sem("attn1_done")
        x_lo_done = sem("x_lo_done")
        h_lo_done = sem("h_lo_done")
        vareps_done = sem("vareps_done")
        rstd_done = sem("rstd_done")

        STEPS = B + LAST
        LOOP0 = LAST + 4
        LOOPS = (B - 2 * PAIR - LOOP0) // BODY
        LOOP1 = LOOP0 + LOOPS * BODY

        def run_steps(eng, step):
            for t in range(LOOP0):
                step(0, t)
            with eng.Fori(0, LOOPS, 1) as i:
                for k in range(LOOP0, LOOP0 + BODY):
                    step(i, k)
            for t in range(LOOP1, STEPS):
                step(0, t)

        def live(t, lag):
            return not isinstance(t, int) or 0 <= t - lag < B

        def begun(t, lag):
            return not isinstance(t, int) or t >= lag

        block = ctx.enter_context(nc.Block())

        @block.sync
        def _(sp):
            def pair_of(ap, q):
                if isinstance(q, int):
                    return ap[q]
                return ap[bass.ds(q, 1)].rearrange("q n k d -> (q n) k d")

            def load_xT(q, k):
                slot = k % (RING // PAIR)
                if k * PAIR >= RING:
                    sp.wait_ge(x_lo_done, q * PAIR + PAIR - RING)
                sp.dma_start(xT_sb[:, slot * PAIR:slot * PAIR + PAIR].rearrange("p g c n -> p g (c n)"),
                             pair_of(xT, q)).then_inc(xT_in[slot], 16)

            def load_adj(q, k):
                slot = k % (RING // PAIR)
                if k * PAIR >= RING:
                    sp.wait_ge(mask_done, q + 1 - RING // PAIR)
                sp.dma_start(adj_sb[:, slot * PAIR:slot * PAIR + PAIR, :], pair_of(adj, q)).then_inc(adj_in[slot], 16)

            def load_x(q, k):
                slot = k % (RING // PAIR)
                if k * PAIR >= RING:
                    sp.wait_ge(resid_done, q * PAIR + PAIR - RING)
                sp.dma_start(x_sb[:, slot * PAIR:slot * PAIR + PAIR, :], pair_of(x, q)).then_inc(x_in[slot], 16)

            def step(i, k):
                t = BODY * i + k
                q = BODY // PAIR * i
                if k % PAIR == 0 and live(t, -2 * PAIR):
                    load_xT(q + k // PAIR + 2, k // PAIR + 2)
                    load_adj(q + k // PAIR + 2, k // PAIR + 2)
                if k % PAIR == 0 and live(t, 0):
                    load_x(q + k // PAIR, k // PAIR)
                if (k - LAST) % PAIR == PAIR - 1 and live(t, LAST):
                    slot = (k - LAST) // PAIR % 2
                    sp.wait_ge(y_done, t - LAST + 1)
                    sp.dma_start(pair_of(out, q + (k - LAST) // PAIR),
                                 y_sb[:, slot * PAIR:slot * PAIR + PAIR, :]).then_inc(y_out[slot], 16)

            load_xT(0, 0)
            for c in range(KC):
                sp.dma_start(w1[:, c, :, 0:HH * F],
                             W1[c * P:(c + 1) * P, :].rearrange("p (j n) -> p j n", j=HG)).then_inc(w1_in, 16)
            load_adj(0, 0)
            load_xT(1, 1)
            load_adj(1, 1)
            run_steps(sp, step)
            for s in y_out:
                sp.wait_ge(s, 16 * (PAIRS // 2))

        @block.gpsimd
        def _(pool):
            nc.gpsimd.memset(ones[:], 1.0).then_inc(consts_ready, 1)
            nc.gpsimd.memset(edge_limit[:], 0.0).then_inc(consts_ready, 1)
            pool.wait_ge(consts_ready, 2)
            nc.gpsimd.affine_select(out=ident[:], in_=ones[:], compare_op=ALU.is_equal, fill=0.0, base=0,
                                    pattern=[[-1, P]], channel_multiplier=1).then_inc(consts_ready, 1)
            nc.gpsimd.affine_select(out=edge_limit[:], in_=edge_limit[:], compare_op=ALU.not_equal, fill=-3e38, base=0,
                                    pattern=[[-1, P]], channel_multiplier=1).then_inc(consts_ready, 1)
            nc.gpsimd.memset(bias1[:], 0.0).then_inc(consts_ready, 1)
            nc.gpsimd.memset(minus_half[:], -0.5).then_inc(consts_ready, 1)
            nc.gpsimd.memset(minus_one[:], -1.0).then_inc(consts_ready, 1)
            nc.gpsimd.memset(ln_eps[:], LN_EPS).then_inc(consts_ready, 1)
            nc.gpsimd.memset(zeros[:], 0.0).then_inc(consts_ready, 1)
            pool.wait_ge(w1_in, 16 * 5)
            for c in range(KC):
                nc.gpsimd.tensor_tensor(prod1[:, 1, c], w1[:, c, :, 0:HH * F], att1[:, 1], ALU.mult).then_inc(prod1_ready, 1)

            def split_x(i, k):
                t = BODY * i + k
                if begun(t, 2):
                    pool.wait_ge(xl_made, t - 1)
                pool.wait_ge(x_hi_done, t + 1)
                nc.gpsimd.tensor_tensor(xT_lo[:, k % 2], xT_sb[:, k % RING], xT_hi[:, k % 2].bitcast(F32),
                                        ALU.subtract).then_inc(x_lo_done, 1)

            def step(i, k):
                t = BODY * i + k
                if live(t, 0):
                    src = xl[:, k % 4, :, HH * F:GW]
                    b = k % 2
                    hi, mid, lo = (parts[:, b, p, :].rearrange("p (j c) -> p j c", j=HG) for p in range(SPLIT))
                    no_shift = zeros[:].rearrange("p (j c) -> p j c", j=HG)
                    rst = rest[:, b, :].rearrange("p (j c) -> p j c", j=HG)
                    pool.wait_ge(xl_done, t + 1)
                    if begun(t, 2):
                        pool.wait_ge(rows_made, t - 1)
                    nc.gpsimd.tensor_tensor(hi, src, no_shift, ALU.add).then_inc(hi_done, 1)
                    pool.wait_ge(hi_done, t + 1)
                    nc.gpsimd.tensor_tensor(rst, src, hi, ALU.subtract).then_inc(rest_done, 1)
                    pool.wait_ge(rest_done, t + 1)
                    nc.gpsimd.tensor_tensor(mid, rst, no_shift, ALU.add).then_inc(mid_done, 1)
                    pool.wait_ge(mid_done, t + 1)
                    nc.gpsimd.tensor_tensor(lo, rst, mid, ALU.subtract).then_inc(parts_done, 1)
                if live(t, 1):
                    b = (k - 1) % 2
                    pool.wait_ge(rden1_done, t)
                    if begun(t, 3):
                        pool.wait_ge(pT_made, t - 2)
                    nc.gpsimd.tensor_tensor(attn1[:, b], prob1[:, b],
                                            rden1[:, b, :].unsqueeze(2).broadcast_to([P, H, P]),
                                            ALU.mult).then_inc(attn1_done, 1)
                if live(t, -1):
                    split_x(i, k + 1)
                if t_is(t, 0):
                    layer2_products()
                if live(t, 2):
                    b = (k - 2) % 2
                    if begun(t, 4):
                        pool.wait_ge(xl2_made, t - 3)
                    pool.wait_ge(h_hi_done, t - 1)
                    nc.gpsimd.tensor_tensor(hT_lo[:, b], hT[:, b], hT_hi[:, b].bitcast(F32), ALU.subtract).then_inc(h_lo_done, 1)
                if live(t, 5):
                    b = (k - 5) % 2
                    pool.wait_ge(meanvar_done, t - 4)
                    nc.gpsimd.tensor_tensor(vareps[:, b:b + 1], meanvar[:, b, 1:2], ln_eps[:], ALU.add).then_inc(vareps_done, 1)
                    pool.wait_ge(vareps_done, t - 4)
                    if begun(t, 7):
                        pool.wait_ge(y_done, t - 6)
                    nc.gpsimd.tensor_tensor(rstd[:, b:b + 1], vareps[:, b:b + 1], minus_half[:],
                                            ALU.pow).then_inc(rstd_done, 1)

            def layer2_products():
                pool.wait_ge(w2_in, 16 * 4)
                for s in range(2):
                    nc.gpsimd.tensor_tensor(prod2[:, s], w2[:, :, 0:DO], att2[:, s, :].unsqueeze(1).broadcast_to([P, H, DO]),
                                            ALU.mult).then_inc(prod2_ready, 1)

            split_x(0, 0)
            run_steps(pool, step)

        @block.scalar
        def _(act):
            act.dma_start(att1[:, 0], att_src1.rearrange("h f -> (h f)").partition_broadcast(P)).then_inc(w1_in, 16)
            act.dma_start(att1[:, 1], att_dst1.rearrange("h f -> (h f)").partition_broadcast(P)).then_inc(w1_in, 16)
            act.dma_start(b1_all[:], b1.partition_broadcast(P)).then_inc(w1_in, 16)
            act.dma_start(w2[:, :, 0:DO], W2.rearrange("(h p) n -> p h n", p=P)).then_inc(w2_in, 16)
            act.dma_start(att2[:, 0, :], att_src2.rearrange("h f -> (h f)").partition_broadcast(P)).then_inc(w2_in, 16)
            act.dma_start(att2[:, 1, :], att_dst2.rearrange("h f -> (h f)").partition_broadcast(P)).then_inc(w2_in, 16)
            act.dma_start(b2_all[:], b2.partition_broadcast(P)).then_inc(w2_in, 16)
            act.wait_ge(consts_ready, 9)

            def step(i, k):
                t = BODY * i + k
                if live(t, 4):
                    b = (k - 4) % 2
                    act.wait_ge(max2_done, t - 3)
                    if begun(t, 6):
                        act.wait_ge(p2T_made, t - 5)
                        act.wait_ge(rden2_done, t - 5)
                    nc.scalar.activation(prob2[:, b], lrelu2[:, b], ACT.Exp, bias=negmax2[:, b:b + 1],
                                         accum_out=den2[:, b:b + 1]).then_inc(prob2_done, 1)
                if live(t, 2):
                    b = (k - 2) % 2
                    act.wait_ge(u_made, t - 1)
                    if begun(t, 4):
                        act.wait_ge(hT_done, t - 3)
                    nc.scalar.activation(expu[:, b], ps_u[:, :, :], ACT.Exp, bias=minus_one[:, 0:1]).then_inc(expu_done, 1)
                if live(t, 0):
                    b = k % 2
                    act.wait_ge(rows_made, t + 1)
                    if begun(t, 2):
                        act.wait_ge(z1_made, t - 1)
                    nc.scalar.copy(score_rows[:, b], ps_rows).then_inc(rows_done, 1)
                if live(t, 4):
                    b = (k - 4) % 2
                    act.wait_ge(p2T_made, t - 3)
                    if begun(t, 6):
                        act.wait_ge(u2_made, t - 5)
                    nc.scalar.copy(prob2T[:, b], ps_p2T).then_inc(prob2T_done, 1)
                if live(t, 0):
                    b = k % 2
                    act.wait_ge(z1_made, t + 1)
                    if begun(t, 2):
                        act.wait_ge(lrelu1_done, t - 1)
                    nc.scalar.copy(score1[:, b], ps_z1[:, :, :]).then_inc(score1_done, 1)
                if live(t, 2):
                    b = (k - 2) % 2
                    act.wait_ge(hT_done, t - 1)
                    if begun(t, 4):
                        act.wait_ge(xl2_made, t - 3)
                    nc.scalar.copy(hT_hi[:, b], hT[:, b]).then_inc(h_hi_done, 1)
                if live(t, 1):
                    b = (k - 1) % 2
                    act.wait_ge(pT_made, t)
                    if begun(t, 3):
                        act.wait_ge(u_made, t - 2)
                    nc.scalar.copy(attn1T[:, b], ps_pT[:, :, :]).then_inc(attn1T_done, 1)
                if live(t, 3):
                    b = (k - 3) % 2
                    act.wait_ge(z2_made, t - 2)
                    if begun(t, 5):
                        act.wait_ge(lrelu2_done, t - 4)
                    nc.scalar.activation(score2[:, b], ps_z2, ACT.Identity, bias=xl2[:, b, DO + 1:DO + 2]).then_inc(score2_done, 1)
                if live(t, 0):
                    b = k % 2
                    act.wait_ge(max1_done, t + 1)
                    if begun(t, 2):
                        act.wait_ge(attn1_done, t - 1)
                    for h in range(H):
                        last = nc.scalar.activation(prob1[:, b, h], lrelu1[:, b, h], ACT.Exp, bias=negmax1[:, b, h:h + 1],
                                                    accum_out=den1[:, b, h:h + 1])
                    last.then_inc(prob1_done, 1)

            run_steps(act, step)

        @block.vector
        def _(dve):
            done = [0]

            def settle(last):
                done[0] += 1
                last.then_inc(setup_step, 1)
                dve.wait_ge(setup_step, done[0])

            def high_x(i, k):
                t = BODY * i + k
                dve.wait_ge(xT_in[k // PAIR % (RING // PAIR)], 16 * (i + k // RING + 1))
                if begun(t, 2):
                    dve.wait_ge(xl_made, t - 1)
                nc.vector.tensor_copy(xT_hi[:, k % 2], xT_sb[:, k % RING]).then_inc(x_hi_done, 1)

            def layer2_weights():
                dve.wait_ge(prod2_ready, 2)
                nc.vector.tensor_reduce(w2[:, :, DO:DO + 1], prod2[:, 0], AX.X, ALU.add)
                settle(nc.vector.tensor_reduce(w2[:, :, DO + 1:DO + 2], prod2[:, 1], AX.X, ALU.add))
                settle(nc.vector.tensor_copy(w2_hi[:], w2[:]))
                nc.vector.tensor_tensor(w2_lo[:], w2[:], w2_hi[:].bitcast(F32), ALU.subtract).then_inc(w2_ready, 1)

            def layer2_bias():
                dve.wait_ge(colsum_ready, 1)
                nc.vector.tensor_tensor(bias2[:, 0:DO], b2_all[:], ps_xl2[:, 0:DO], ALU.subtract).then_inc(bias2_ready, 1)
                nc.vector.tensor_scalar(bias2[:, DO:W2C], ps_xl2[:, DO:W2C], -1.0, None, ALU.mult).then_inc(bias2_ready, 1)
                dve.wait_ge(bias2_ready, 2)

            def step(i, k):
                t = BODY * i + k
                if live(t, 0):
                    dve.wait_ge(xl_made, t + 1)
                    if begun(t, 4):
                        dve.wait_ge(u_made, t - 3)
                    nc.vector.tensor_tensor(xl[:, k % 4], ps_xl[:, :, 0:GW], bias1[:], ALU.add).then_inc(xl_done, 1)
                if live(t, -1):
                    high_x(i, k + 1)
                if live(t, 1):
                    b = (k - 1) % 2
                    dve.wait_ge(prob1_done, t)
                    if begun(t, 3):
                        dve.wait_ge(attn1_done, t - 2)
                    nc.vector.reciprocal(rden1[:, b], den1[:, b]).then_inc(rden1_done, 1)
                if live(t, 5):
                    b = (k - 5) % 2
                    dve.wait_ge(x_in[(k - 5) // PAIR % (RING // PAIR)], 16 * (i + (k - 5) // RING + 1))
                    dve.wait_ge(rden2_done, t - 4)
                    dve.wait_ge(u2_made, t - 4)
                    if begun(t, 7):
                        dve.wait_ge(y_done, t - 6)
                    nc.vector.scalar_tensor_tensor(resid[:, b], ps_u2, rden2[:, b:b + 1], x_sb[:, (k - 5) % RING],
                                                   ALU.mult, ALU.add).then_inc(resid_done, 1)
                    dve.wait_ge(resid_done, t - 4)
                    nc.vector.bn_stats(stats[:, b], resid[:, b]).then_inc(stats_done, 1)
                if live(t, 4):
                    b = (k - 4) % 2
                    dve.wait_ge(prob2_done, t - 3)
                    nc.vector.reciprocal(rden2[:, b:b + 1], den2[:, b:b + 1]).then_inc(rden2_done, 1)
                if live(t, 2):
                    b = (k - 2) % 2
                    dve.wait_ge(expu_done, t - 1)
                    if begun(t, 4):
                        dve.wait_ge(h_lo_done, t - 3)
                    nc.vector.scalar_tensor_tensor(hT[:, b], expu[:, b], 1.0, ps_u[:, :, :], ALU.min, ALU.max).then_inc(hT_done, 1)
                if t_is(t, 2):
                    layer2_bias()
                if live(t, 5):
                    dve.wait_ge(stats_done, t - 4)
                if live(t, 3):
                    b = (k - 3) % 2
                    dve.wait_ge(xl2_made, t - 2)
                    if begun(t, 5):
                        dve.wait_ge(u2_made, t - 4)
                    nc.vector.tensor_tensor(xl2[:, b], ps_xl2[:, 0:W2C], bias2[:], ALU.add).then_inc(xl2_done, 1)
                if live(t, 5):
                    b = (k - 5) % 2
                    nc.vector.bn_aggr(meanvar[:, b], stats[:, b]).then_inc(meanvar_done, 1)
                if k % PAIR == 1 and live(t, -1):
                    make_masks(i, k + 1)
                if live(t, 0):
                    b = k % 2
                    dve.wait_ge(score1_done, t + 1)
                    if begun(t, 2):
                        dve.wait_ge(prob1_done, t - 1)
                    nc.vector.scalar_tensor_tensor(lrelu1[:, b], score1[:, b], NEG_SLOPE, ps_z1[:, :, :], ALU.mult,
                                                   ALU.max).then_inc(lrelu1_done, 1)
                    dve.wait_ge(lrelu1_done, t + 1)
                    nc.vector.tensor_reduce(negmax1[:, b], lrelu1[:, b], AX.X, ALU.max, negate=True).then_inc(max1_done, 1)
                if live(t, 3):
                    b = (k - 3) % 2
                    dve.wait_ge(score2_done, t - 2)
                    if begun(t, 5):
                        dve.wait_ge(prob2_done, t - 4)
                    nc.vector.scalar_tensor_tensor(lrelu2[:, b], score2[:, b], NEG_SLOPE, score2[:, b], ALU.mult,
                                                   ALU.max).then_inc(lrelu2_done, 1)
                if live(t, 6):
                    b, slot = (k - 6) % 2, (k - 6) % 4
                    dve.wait_ge(rstd_done, t - 5)
                    if begun(t, 10):
                        dve.wait_ge(y_out[slot // PAIR], 16 * (BODY // 4 * i + (k - 6) // 4))
                    nc.vector.tensor_scalar(y_sb[:, slot, :], resid[:, b, :], meanvar[:, b, 0:1], rstd[:, b:b + 1],
                                            ALU.subtract, ALU.mult).then_inc(y_done, 1)
                if live(t, 3):
                    b = (k - 3) % 2
                    dve.wait_ge(lrelu2_done, t - 2)
                    nc.vector.tensor_reduce(negmax2[:, b:b + 1], lrelu2[:, b], AX.X, ALU.max, negate=True).then_inc(max2_done, 1)
                if t_is(t, 1):
                    layer2_weights()

            def make_masks(i, k):
                t = BODY * i + k
                slot = k % RING
                dve.wait_ge(adj_in[slot // PAIR], 16 * (i + k // RING + 1))
                if begun(t, RING):
                    dve.wait_ge(z2_made, t + PAIR - RING)
                nc.vector.tensor_tensor(no_edge[:, slot:slot + PAIR, :], adj_sb[:, slot:slot + PAIR, :],
                                        edge_limit[:].unsqueeze(1).broadcast_to([P, PAIR, P]), ALU.is_le).then_inc(mask_done, 1)

            dve.wait_ge(consts_ready, 9)
            nc.vector.tensor_copy(ident_bf[:], ident[:])
            nc.vector.tensor_scalar(mask_ident[:], ident[:].unsqueeze(1).broadcast_to([P, H, P]), MASKED, None, ALU.mult)
            settle(nc.vector.tensor_reduce(row_sel[:], ident[0:R, 0:R].rearrange("r (p c) -> r c p", c=NS), AX.X, ALU.add))
            chosen = row_sel[:].rearrange("r (j s h) -> r j s h", j=HG, s=2)
            for s, sel in ((0, sel_src), (1, sel_dst)):
                for j in range(HG):
                    nc.vector.tensor_copy(sel[:, j * HH:(j + 1) * HH, :], chosen[:, j, s, :].unsqueeze(2).broadcast_to([R, HH, P]))
            high_x(0, 0)
            make_masks(0, 0)
            dve.wait_ge(w1_in, 16 * 5)
            for c in range(KC):
                last = nc.vector.tensor_tensor(prod1[:, 0, c], w1[:, c, :, 0:HH * F], att1[:, 0], ALU.mult)
            settle(last)
            dve.wait_ge(prod1_ready, KC)
            for s in range(2):
                for c in range(KC):
                    last = nc.vector.tensor_reduce(w1[:, c, :, HH * F + s * HH:HH * F + (s + 1) * HH],
                                                   prod1[:, s, c].rearrange("p j (h f) -> p j h f", f=F), AX.X, ALU.add)
            settle(last)
            settle(nc.vector.tensor_copy(w1_hi[:], w1[:]))
            nc.vector.tensor_tensor(w1_lo[:], w1[:], w1_hi[:].bitcast(F32), ALU.subtract).then_inc(w1_ready, 1)
            settle(nc.vector.tensor_scalar(bias1[:, :, 0:HH * F], b1_all[:].rearrange("p (j n) -> p j n", j=HG), 1.0, None,
                                           ALU.add))
            run_steps(dve, step)

        @block.tensor
        def _(pe):
            def step(i, k):
                t = BODY * i + k
                if live(t, 0):
                    pe.wait_ge(x_lo_done, t + 1)
                    if begun(t, 1):
                        pe.wait_ge(xl_done, t)
                    for j in range(HG):
                        for c in range(KC):
                            x_hi, x_lo, w_hi, w_lo = xT_hi[:, k % 2, c, :], xT_lo[:, k % 2, c, :], w1_hi[:, c, j, :], w1_lo[:, c, j, :]
                            nc.tensor.matmul(ps_xl[:, j, 0:GW], x_hi, w_hi, start=(c == 0), stop=False)
                            nc.tensor.matmul(ps_xl[:, j, 0:GW], x_hi, w_lo, start=False, stop=False)
                            last = nc.tensor.matmul(ps_xl[:, j, 0:GW], x_lo, w_hi, start=False, stop=(c == KC - 1))
                    last.then_inc(xl_made, 1)
                if live(t, 2):
                    b = (k - 2) % 2
                    pe.wait_ge(attn1T_done, t - 1)
                    if begun(t, 3):
                        pe.wait_ge(hT_done, t - 2)
                    for h in range(H):
                        j, hh = h // HH, h % HH
                        last = nc.tensor.matmul(ps_u[:, h, :], xl[:, (k - 2) % 4, j, hh * F:(hh + 1) * F], attn1T[:, b, h],
                                                start=True, stop=True)
                    last.then_inc(u_made, 1)
                if t_is(t, 3):
                    pe.wait_ge(bias2_ready, 2)
                if live(t, 3):
                    pe.wait_ge(h_lo_done, t - 2)
                    if begun(t, 4):
                        pe.wait_ge(xl2_done, t - 3)
                    for h in range(H - 1):
                        product2((k - 3) % 2, h)
                if live(t, 0):
                    pe.wait_ge(parts_done, t + 1)
                    if begun(t, 4):
                        pe.wait_ge(score2_done, t - 3)
                    nc.tensor.transpose(ps_rows, parts[:, k % 2].rearrange("p a b -> p (a b)"), ident_bf[:]).then_inc(rows_made, 1)
                if live(t, 4):
                    b = (k - 4) % 2
                    pe.wait_ge(prob2_done, t - 3)
                    if begun(t, 5):
                        pe.wait_ge(resid_done, t - 4)
                    nc.tensor.transpose(ps_p2T, prob2[:, b], ident[:]).then_inc(p2T_made, 1)
                if live(t, 3):
                    product2((k - 3) % 2, H - 1).then_inc(xl2_made, 1)
                if live(t, 0):
                    b = k % 2
                    pe.wait_ge(mask_done, BODY // PAIR * i + k // PAIR + 1)
                    pe.wait_ge(rows_done, t + 1)
                    if begun(t, 1):
                        pe.wait_ge(lrelu1_done, t)
                    z = ps_z1[:].rearrange("p h d -> p (h d)")
                    nc.tensor.matmul(z, no_edge[:, k % RING], mask_ident[:].rearrange("p h d -> p (h d)"), start=True, stop=False)
                    nc.tensor.matmul(z, score_rows[:, b], sel_dst[:].rearrange("p h d -> p (h d)"), start=False, stop=False)
                    for h in range(H):
                        last = nc.tensor.matmul(ps_z1[:, h, :], sel_src[:, h], score_rows[:, b], start=False, stop=(h == H - 1))
                    last.then_inc(z1_made, 1)
                if live(t, 4):
                    b = (k - 4) % 2
                    pe.wait_ge(prob2T_done, t - 3)
                    nc.tensor.matmul(ps_u2, prob2T[:, b], xl2[:, b, 0:DO], start=True, stop=True).then_inc(u2_made, 1)
                if live(t, 1):
                    b = (k - 1) % 2
                    pe.wait_ge(attn1_done, t)
                    if begun(t, 2):
                        pe.wait_ge(attn1T_done, t - 1)
                    for h in range(H):
                        last = nc.tensor.transpose(ps_pT[:, h, :], attn1[:, b, h], ident[:])
                    last.then_inc(pT_made, 1)
                if live(t, 3):
                    b = (k - 3) % 2
                    pe.wait_ge(xl2_done, t - 2)
                    if begun(t, 3) and live(t, 0):
                        pe.wait_ge(rows_done, t + 1)
                    if begun(t, 4):
                        pe.wait_ge(score2_done, t - 3)
                    nc.tensor.matmul(ps_z2, no_edge[:, (k - 3) % RING], mask_ident[:, 0, :], start=True, stop=False)
                    nc.tensor.matmul(ps_z2, xl2[:, b, DO:DO + 1].broadcast_to([P, P]), ident[:],
                                     start=False, stop=True).then_inc(z2_made, 1)
                if t_is(t, 1):
                    layer2_column_sums()

            def product2(b, h):
                h_hi, h_lo, w_hi, w_lo = hT_hi[:, b, h], hT_lo[:, b, h], w2_hi[:, h, :], w2_lo[:, h, :]
                nc.tensor.matmul(ps_xl2[:, 0:W2C], h_hi, w_hi, start=(h == 0), stop=False)
                nc.tensor.matmul(ps_xl2[:, 0:W2C], h_hi, w_lo, start=False, stop=False)
                return nc.tensor.matmul(ps_xl2[:, 0:W2C], h_lo, w_hi, start=False, stop=(h == H - 1))

            def layer2_column_sums():
                pe.wait_ge(w2_ready, 1)
                for h in range(H):
                    last = nc.tensor.matmul(ps_xl2[:, 0:W2C], ones[:], w2[:, h, :], start=(h == 0), stop=(h == H - 1))
                last.then_inc(colsum_ready, 1)

            pe.wait_ge(consts_ready, 9)
            pe.wait_ge(w1_ready, 1)
            run_steps(pe, step)


def t_is(t, number):
    return isinstance(t, int) and t == number


_WEIGHTS = ['L0_gnn_W1', 'L0_gnn_att_src1', 'L0_gnn_att_dst1', 'L0_gnn_b1', 'L0_gnn_W2', 'L0_gnn_att_src2',
            'L0_gnn_att_dst2', 'L0_gnn_b2']


def kernel(**inputs):
    import numpy as _np
    import concourse.bacc as _bacc
    from concourse import mybir as _mybir
    from concourse.bass_utils import run_bass_kernel_spmd as _run

    nc = _bacc.Bacc("TRN2", target_bir_lowering=False, num_devices=1)
    x, adj = _np.asarray(inputs['x']), _np.asarray(inputs['adj'])
    B, N, D = x.shape
    laid = {
        'x': x.reshape(B // 2, 2, N, D).transpose(0, 2, 1, 3),
        'xT': x.reshape(B // 2, 2, N, D // P, P).transpose(0, 4, 1, 3, 2).reshape(B // 2, P, 2, -1),
        'adj': adj.reshape(B // 2, 2, N, N).transpose(0, 2, 1, 3),
    }
    for name in _WEIGHTS:
        laid[name] = _np.asarray(inputs[name])
    arrays, args = {}, []
    for name, a in laid.items():
        a = _np.ascontiguousarray(a)
        arrays[f"in_{name}_dram"] = a
        args.append(nc.dram_tensor(f"in_{name}_dram", a.shape, _mybir.dt.from_np(a.dtype), kind="ExternalInput").ap())
    args.append(nc.dram_tensor("out_0_dram", (B // 2, N, 2, D), _mybir.dt.float32, kind="ExternalOutput").ap())
    gat_block_program(nc, *args)
    r = _run(nc, [arrays], core_ids=[0])
    return r.results[0]["out_0_dram"].transpose(0, 2, 1, 3).reshape(B, N, D)
```

```python
from contextlib import ExitStack

import concourse.bass as bass
from concourse import mybir

P = 128
ALU = mybir.AluOpType
ACT = mybir.ActivationFunctionType
AX = mybir.AxisListType
F32 = mybir.dt.float32
F32R = mybir.dt.float32r
BF16 = mybir.dt.bfloat16
I32 = mybir.dt.int32

NEG_SLOPE = 0.2
LN_EPS = 1e-5
MASKED = -(2.0 ** 100)


def gat_block_program(nc, x, xT, adj, W1, W1T, att1_cols, b1, W2, att2_b2, out):
    PAIRS, N, PAIR, D = x.shape
    B = PAIRS * PAIR
    F, H, _ = att1_cols.shape
    HF = H * F
    DO = W2.shape[1]
    assert N == P and F == P and D % P == 0 and DO == D
    KC = D // P
    HG = 2
    HH = H // HG
    GW = HH * F + 2 * HH
    NS = 2 * H
    SPLIT = 3
    Q = 32
    assert SPLIT * H <= Q
    POS = 1 / NEG_SLOPE - 1
    W2C = DO + 2
    RING = 8
    BODY = 3 * RING
    EARLY = H - 1
    LAST = 6

    ctx = ExitStack()
    with ctx:
        def sb(name, shape, dt=F32):
            return ctx.enter_context(nc.sbuf_tensor(name, shape, dt))

        def psum(name, shape, dt=F32):
            return ctx.enter_context(nc.psum_tensor(name, shape, dt))

        def sem(name):
            return ctx.enter_context(nc.semaphore(name))

        w1 = sb("w1", [P, KC, HG, HH * F])
        w1_hi = sb("w1_hi", [P, KC, HG, GW], F32R)
        w1_lo = sb("w1_lo", [P, KC, HG, GW], F32R)
        w1T = sb("w1T", [P, H, KC, P])
        w2 = sb("w2", [P, H, W2C])
        w2_hi = sb("w2_hi", [P, H, W2C], F32R)
        w2_lo = sb("w2_lo", [P, H, W2C], F32R)
        bias1 = sb("bias1", [P, HG, HH * F])
        bias2 = sb("bias2", [P, W2C])
        att1 = sb("att1", [P, H, 2])
        b1_all = sb("b1_all", [P, HG, HH * F])
        att2_all = sb("att2_all", [P, 3, DO])
        prod2 = sb("prod2", [P, 2, H, DO])
        ones_r = sb("ones_r", [P, P], F32R)
        ones = sb("ones", [P, P])
        ident = sb("ident", [P, P])
        ident_bf = sb("ident_bf", [P, P], BF16)
        mask_ident = sb("mask_ident", [P, H, P], BF16)
        edge_limit = sb("edge_limit", [P, P])
        part_of = sb("part_of", [2 * Q, H])
        any_part = sb("any_part", [Q, 1])
        src_of = sb("src_of", [Q, H, P], BF16)
        minus_half = sb("minus_half", [P, 1])
        ln_eps = sb("ln_eps", [P, 1])
        zeros = sb("zeros", [P, NS])
        minus_one = sb("minus_one", [P, 1])

        x_sb = sb("x_sb", [P, RING, D])
        xT_sb = sb("xT_sb", [P, RING, KC, P])
        adj_sb = sb("adj_sb", [P, RING, P], I32)
        no_edge = sb("no_edge", [P, RING, P], BF16)
        xT_hi = sb("xT_hi", [P, 2, KC, P], F32R)
        xT_lo = sb("xT_lo", [P, 2, KC, P], F32R)
        xl = sb("xl", [P, 4, HG, GW])
        parts = sb("parts", [P, 2, P // Q, Q], BF16)
        rest = sb("rest", [P, 2, NS])
        src_rows = sb("src_rows", [Q, 2, P], BF16)
        pair_left = sb("pair_left", [2 * Q, 2, P], BF16)
        pair_right = sb("pair_right", [2 * Q, 2, H, P], BF16)
        pos1 = sb("pos1", [P, 2, H, P])
        neg_lrelu1 = sb("neg_lrelu1", [P, 2, H, P])
        negmax1 = sb("negmax1", [P, 2, H])
        prob1 = sb("prob1", [P, 2, H, P])
        den1 = sb("den1", [P, 2, H])
        rden1 = sb("rden1", [P, 2, H])
        attn1 = sb("attn1", [P, 2, H, P])
        attn1T = sb("attn1T", [P, 2, H, P])
        expu = sb("expu", [P, 2, H, P])
        hT = sb("hT", [P, 2, H, P])
        hT_hi = sb("hT_hi", [P, 2, H, P], F32R)
        hT_lo = sb("hT_lo", [P, 2, H, P], F32R)
        xl2 = sb("xl2", [P, 2, W2C])
        score2 = sb("score2", [P, 2, P])
        lrelu2 = sb("lrelu2", [P, 2, P])
        negmax2 = sb("negmax2", [P, 2])
        prob2 = sb("prob2", [P, 2, P])
        den2 = sb("den2", [P, 2])
        rden2 = sb("rden2", [P, 2])
        prob2T = sb("prob2T", [P, 2, P])
        resid = sb("resid", [P, 2, D])
        stats = sb("stats", [P, 2, 6])
        meanvar = sb("meanvar", [P, 2, 2])
        vareps = sb("vareps", [P, 2])
        rstd = sb("rstd", [P, 2])
        y_sb = sb("y_sb", [P, 4, D])

        ps_small = psum("ps_small", [P, 512])
        ps_xl = psum("ps_xl", [P, HG, 512])
        ps_z1 = psum("ps_z1", [P, H, P])
        ps_pT = psum("ps_pT", [P, H, P])
        ps_u = psum("ps_u", [P, H, P])
        ps_xl2 = psum("ps_xl2", [P, 512])
        ps_l2 = psum("ps_l2", [P, 512])
        ps_z2 = ps_small[:, 0:P]
        ps_rows = ps_small[:, 0:P].bitcast(BF16)[:, 0:P]
        ps_p2T = ps_l2[:, 0:P]
        ps_u2 = ps_l2[:, 0:DO]
        ps_w1_scores = ps_l2[:, 0:KC * NS].rearrange("p (c j n) -> p c j n", c=KC, j=HG)

        w1_in = sem("w1_in")
        w1T_in = sem("w1T_in")
        b1_in = sem("b1_in")
        w2_in = sem("w2_in")
        consts_ready = sem("consts_ready")
        mask_ident_ready = sem("mask_ident_ready")
        w1_hi_ready = sem("w1_hi_ready")
        w1_ready = sem("w1_ready")
        w1_scores_made = sem("w1_scores_made")
        w2_scores_ready = sem("w2_scores_ready")
        w2_hi_ready = sem("w2_hi_ready")
        w2_ready = sem("w2_ready")
        colsum_made = sem("colsum_made")
        bias2_ready = sem("bias2_ready")
        setup_step = sem("setup_step")
        x_in = [sem(f"x_in{k}") for k in range(RING // PAIR)]
        xT_in = [sem(f"xT_in{k}") for k in range(RING // PAIR)]
        adj_in = [sem(f"adj_in{k}") for k in range(RING // PAIR)]
        y_out = [sem(f"y_out{k}") for k in range(2)]
        xl_made = sem("xl_made")
        rows_made = sem("rows_made")
        z1_made = sem("z1_made")
        pT_made = sem("pT_made")
        u_made = sem("u_made")
        xl2_made = sem("xl2_made")
        z2_made = sem("z2_made")
        p2T_made = sem("p2T_made")
        u2_made = sem("u2_made")
        pos1_done = sem("pos1_done")
        prob1_done = sem("prob1_done")
        attn1T_done = sem("attn1T_done")
        rows_done = sem("rows_done")
        expu_done = sem("expu_done")
        h_hi_done = sem("h_hi_done")
        score2_done = sem("score2_done")
        prob2_done = sem("prob2_done")
        prob2T_done = sem("prob2T_done")
        mask_done = sem("mask_done")
        x_hi_done = sem("x_hi_done")
        scores_done = sem("scores_done")
        xl_done = sem("xl_done")
        src_pairs_done = sem("src_pairs_done")
        lrelu2_done = sem("lrelu2_done")
        max1_done = sem("max1_done")
        rden1_done = sem("rden1_done")
        hT_done = sem("hT_done")
        xl2_done = sem("xl2_done")
        max2_done = sem("max2_done")
        rden2_done = sem("rden2_done")
        resid_done = sem("resid_done")
        stats_done = sem("stats_done")
        meanvar_done = sem("meanvar_done")
        y_done = sem("y_done")
        rest_done = sem("rest_done")
        mid_done = sem("mid_done")
        parts_done = sem("parts_done")
        attn1_done = sem("attn1_done")
        x_lo_done = sem("x_lo_done")
        h_lo_done = sem("h_lo_done")
        vareps_done = sem("vareps_done")
        rstd_done = sem("rstd_done")

        STEPS = B + LAST
        LOOP0 = LAST + 4
        LOOPS = (B - 2 * PAIR - LOOP0) // BODY
        LOOP1 = LOOP0 + LOOPS * BODY

        def run_steps(eng, step):
            for t in range(LOOP0):
                step(0, t)
            with eng.Fori(0, LOOPS, 1) as i:
                for k in range(LOOP0, LOOP0 + BODY):
                    step(i, k)
            for t in range(LOOP1, STEPS):
                step(0, t)

        def live(t, lag):
            return not isinstance(t, int) or 0 <= t - lag < B

        def begun(t, lag):
            return not isinstance(t, int) or t >= lag

        block = ctx.enter_context(nc.Block())

        @block.sync
        def _(sp):
            def pair_of(ap, q):
                if isinstance(q, int):
                    return ap[q]
                return ap[bass.ds(q, 1)].rearrange("q n k d -> (q n) k d")

            def load_xT(q, k):
                slot = k % (RING // PAIR)
                if k * PAIR >= RING:
                    sp.wait_ge(x_lo_done, q * PAIR + PAIR - RING)
                sp.dma_start(xT_sb[:, slot * PAIR:slot * PAIR + PAIR].rearrange("p g c n -> p g (c n)"),
                             pair_of(xT, q)).then_inc(xT_in[slot], 16)

            def load_adj(q, k):
                slot = k % (RING // PAIR)
                if k * PAIR >= RING:
                    sp.wait_ge(mask_done, q * PAIR + PAIR - RING)
                sp.dma_start(adj_sb[:, slot * PAIR:slot * PAIR + PAIR, :], pair_of(adj, q)).then_inc(adj_in[slot], 16)

            def load_x(q, k):
                slot = k % (RING // PAIR)
                if k * PAIR >= RING:
                    sp.wait_ge(resid_done, q * PAIR + PAIR - RING)
                sp.dma_start(x_sb[:, slot * PAIR:slot * PAIR + PAIR, :], pair_of(x, q)).then_inc(x_in[slot], 16)

            def step(i, k):
                t = BODY * i + k
                q = BODY // PAIR * i
                if k % PAIR == 0 and live(t, -2 * PAIR):
                    load_xT(q + k // PAIR + 2, k // PAIR + 2)
                    load_adj(q + k // PAIR + 2, k // PAIR + 2)
                if k % PAIR == 0 and live(t, 0):
                    load_x(q + k // PAIR, k // PAIR)
                if (k - LAST) % PAIR == PAIR - 1 and live(t, LAST):
                    slot = (k - LAST) // PAIR % 2
                    sp.wait_ge(y_done, t - LAST + 1)
                    sp.dma_start(pair_of(out, q + (k - LAST) // PAIR),
                                 y_sb[:, slot * PAIR:slot * PAIR + PAIR, :]).then_inc(y_out[slot], 16)

            sp.dma_start(w1T[:].rearrange("p h c k -> p (h c k)"), W1T).then_inc(w1T_in, 16)
            load_xT(0, 0)
            load_adj(0, 0)
            sp.dma_start(w2[:, :, 0:DO], W2.rearrange("(h p) n -> p h n", p=P)).then_inc(w2_in, 16)
            load_xT(1, 1)
            load_adj(1, 1)
            run_steps(sp, step)
            for s in y_out:
                sp.wait_ge(s, 16 * (PAIRS // 2))

        @block.gpsimd
        def _(pool):
            nc.gpsimd.memset(ones[:], 1.0).then_inc(consts_ready, 1)
            nc.gpsimd.memset(edge_limit[:], 0.0).then_inc(consts_ready, 1)
            pool.wait_ge(consts_ready, 2)
            nc.gpsimd.affine_select(out=ident[:], in_=ones[:], compare_op=ALU.is_equal, fill=0.0, base=0,
                                    pattern=[[-1, P]], channel_multiplier=1).then_inc(consts_ready, 1)
            nc.gpsimd.affine_select(out=edge_limit[:], in_=edge_limit[:], compare_op=ALU.not_equal, fill=-3e38, base=0,
                                    pattern=[[-1, P]], channel_multiplier=1).then_inc(consts_ready, 1)
            nc.gpsimd.memset(minus_half[:], -0.5).then_inc(consts_ready, 1)
            nc.gpsimd.memset(minus_one[:], -1.0).then_inc(consts_ready, 1)
            nc.gpsimd.memset(ln_eps[:], LN_EPS).then_inc(consts_ready, 1)
            nc.gpsimd.memset(zeros[:], 0.0).then_inc(consts_ready, 1)
            nc.gpsimd.memset(parts[:], 0.0).then_inc(consts_ready, 1)
            pool.wait_ge(consts_ready, 9)
            pool.wait_ge(w1_hi_ready, 1)
            nc.gpsimd.tensor_tensor(w1_lo[:, KC - 1, HG - 1, 0:HH * F], w1[:, KC - 1, HG - 1],
                                    w1_hi[:, KC - 1, HG - 1, 0:HH * F].bitcast(F32), ALU.subtract).then_inc(w1_ready, 1)

            def split_x(i, k):
                t = BODY * i + k
                if begun(t, 2):
                    pool.wait_ge(xl_made, t - 1)
                pool.wait_ge(x_hi_done, t + 1)
                nc.gpsimd.tensor_tensor(xT_lo[:, k % 2], xT_sb[:, k % RING], xT_hi[:, k % 2].bitcast(F32),
                                        ALU.subtract).then_inc(x_lo_done, 1)

            def step(i, k):
                t = BODY * i + k
                if live(t, 0):
                    by_group = lambda ap: ap.rearrange("p (j s h) -> p j s h", j=HG, s=2)
                    b = k % 2
                    score = xl[:, k % 4, :, HH * F:GW].rearrange("p j (s h) -> p j s h", s=2)
                    hi, mid, lo = (parts[:, b, 0:2, p * H:(p + 1) * H].rearrange("p s (j h) -> p j s h", j=HG) for p in range(SPLIT))
                    no_shift, rst = by_group(zeros[:]), by_group(rest[:, b, :])
                    pool.wait_ge(scores_done, t + 1)
                    nc.gpsimd.tensor_tensor(rst, score, hi, ALU.subtract).then_inc(rest_done, 1)
                    pool.wait_ge(rest_done, t + 1)
                    nc.gpsimd.tensor_tensor(mid, rst, no_shift, ALU.add).then_inc(mid_done, 1)
                    pool.wait_ge(mid_done, t + 1)
                    nc.gpsimd.tensor_tensor(lo, rst, mid, ALU.subtract).then_inc(parts_done, 1)
                if live(t, 1):
                    b = (k - 1) % 2
                    pool.wait_ge(rden1_done, t)
                    if begun(t, 3):
                        pool.wait_ge(pT_made, t - 2)
                    nc.gpsimd.tensor_tensor(attn1[:, b], prob1[:, b],
                                            rden1[:, b, :].unsqueeze(2).broadcast_to([P, H, P]),
                                            ALU.mult).then_inc(attn1_done, 1)
                if live(t, -1):
                    split_x(i, k + 1)
                if t_is(t, 0):
                    pool.wait_ge(w2_hi_ready, 1)
                    layer2_low(slice(0, DO))
                    pool.wait_ge(w2_hi_ready, 2)
                    layer2_low(slice(DO, W2C))
                if live(t, 0):
                    deviation(i, k)
                    split_h(i, k)
                else:
                    split_h(i, k)
                    deviation(i, k)

            def deviation(i, k):
                t = BODY * i + k
                if live(t, 5):
                    b = (k - 5) % 2
                    pool.wait_ge(meanvar_done, t - 4)
                    nc.gpsimd.tensor_tensor(vareps[:, b:b + 1], meanvar[:, b, 1:2], ln_eps[:], ALU.add).then_inc(vareps_done, 1)
                    pool.wait_ge(vareps_done, t - 4)
                    if begun(t, 7):
                        pool.wait_ge(y_done, t - 6)
                    nc.gpsimd.tensor_tensor(rstd[:, b:b + 1], vareps[:, b:b + 1], minus_half[:],
                                            ALU.pow).then_inc(rstd_done, 1)

            def split_h(i, k):
                t = BODY * i + k
                if live(t, 2):
                    b = (k - 2) % 2
                    if begun(t, 4):
                        pool.wait_ge(xl2_made, t - 3)
                    pool.wait_ge(h_hi_done, t - 1)
                    nc.gpsimd.tensor_tensor(hT_lo[:, b], hT[:, b], hT_hi[:, b].bitcast(F32), ALU.subtract).then_inc(h_lo_done, 1)

            def layer2_low(columns):
                nc.gpsimd.tensor_tensor(w2_lo[:, :, columns], w2[:, :, columns], w2_hi[:, :, columns].bitcast(F32),
                                        ALU.subtract).then_inc(w2_ready, 1)

            split_x(0, 0)
            run_steps(pool, step)

        @block.scalar
        def _(act):
            act.dma_start(att1[:], att1_cols).then_inc(w1T_in, 16)
            act.dma_start(w1[:].rearrange("p c j n -> p c (j n)"), W1.rearrange("(c p) n -> p c n", p=P)).then_inc(w1_in, 16)
            act.dma_start(b1_all[:].rearrange("p j n -> p (j n)"), b1.partition_broadcast(P)).then_inc(b1_in, 16)
            act.dma_start(att2_all[:].rearrange("p v n -> p (v n)"),
                          att2_b2.partition_broadcast(P)).then_inc(w2_in, 16)
            act.wait_ge(consts_ready, 9)
            nc.scalar.mul(mask_ident[:], ident[:].unsqueeze(1).broadcast_to([P, H, P]), MASKED).then_inc(mask_ident_ready, 1)

            def step(i, k):
                t = BODY * i + k
                if live(t, 0):
                    b = k % 2
                    act.wait_ge(rows_made, t + 1)
                    if begun(t, 2):
                        act.wait_ge(z1_made, t - 1)
                        act.wait_ge(src_pairs_done, t - 1)
                    nc.scalar.copy(src_rows[:, b], ps_rows[0:Q]).then_inc(rows_done, 1)
                    nc.scalar.copy(pair_left[Q:2 * Q, b], ps_rows[Q:2 * Q]).then_inc(rows_done, 1)
                if live(t, 2):
                    b = (k - 2) % 2
                    act.wait_ge(u_made, t - 1)
                    if begun(t, 4):
                        act.wait_ge(hT_done, t - 3)
                    nc.scalar.activation(expu[:, b], ps_u[:, :, :], ACT.Exp, bias=minus_one[:, 0:1]).then_inc(expu_done, 1)
                if live(t, 4):
                    b = (k - 4) % 2
                    act.wait_ge(p2T_made, t - 3)
                    if begun(t, 6):
                        act.wait_ge(u2_made, t - 5)
                    nc.scalar.copy(prob2T[:, b], ps_p2T).then_inc(prob2T_done, 1)
                if live(t, 0):
                    b = k % 2
                    act.wait_ge(z1_made, t + 1)
                    if begun(t, 2):
                        act.wait_ge(max1_done, t - 1)
                    nc.scalar.activation(pos1[:, b], ps_z1[:, :, :], ACT.Relu, scale=POS).then_inc(pos1_done, 1)
                if t_is(t, 0):
                    act.wait_ge(w2_scores_ready, 2 * H)
                    nc.scalar.copy(w2_hi[:, :, DO:W2C], w2[:, :, DO:W2C]).then_inc(w2_hi_ready, 1)
                if live(t, 2):
                    b = (k - 2) % 2
                    act.wait_ge(hT_done, t - 1)
                    if begun(t, 4):
                        act.wait_ge(xl2_made, t - 3)
                    nc.scalar.copy(hT_hi[:, b], hT[:, b]).then_inc(h_hi_done, 1)
                if live(t, 0):
                    pairs2_out(i, k)
                    attn1T_out(i, k)
                else:
                    attn1T_out(i, k)
                    pairs2_out(i, k)
                if live(t, 0):
                    b = k % 2
                    act.wait_ge(max1_done, t + 1)
                    if begun(t, 2):
                        act.wait_ge(attn1_done, t - 1)
                    for h in range(H // 2):
                        exp_head(b, h)
                if live(t, 3):
                    b = (k - 3) % 2
                    act.wait_ge(max2_done, t - 2)
                    if begun(t, 5):
                        act.wait_ge(p2T_made, t - 4)
                        act.wait_ge(rden2_done, t - 4)
                    nc.scalar.activation(prob2[:, b], lrelu2[:, b], ACT.Exp, bias=negmax2[:, b:b + 1],
                                         accum_out=den2[:, b:b + 1]).then_inc(prob2_done, 1)
                if live(t, 0):
                    for h in range(H // 2, H):
                        last = exp_head(k % 2, h)
                    last.then_inc(prob1_done, 1)

            def pairs2_out(i, k):
                t = BODY * i + k
                if live(t, 3):
                    b = (k - 3) % 2
                    act.wait_ge(z2_made, t - 2)
                    if begun(t, 5):
                        act.wait_ge(lrelu2_done, t - 4)
                    nc.scalar.activation(score2[:, b], ps_z2, ACT.Identity, bias=xl2[:, b, DO + 1:DO + 2]).then_inc(score2_done, 1)

            def attn1T_out(i, k):
                t = BODY * i + k
                if live(t, 1):
                    b = (k - 1) % 2
                    act.wait_ge(pT_made, t)
                    if begun(t, 3):
                        act.wait_ge(u_made, t - 2)
                    nc.scalar.copy(attn1T[:, b], ps_pT[:, :, :]).then_inc(attn1T_done, 1)

            def exp_head(b, h):
                return nc.scalar.activation(prob1[:, b, h], neg_lrelu1[:, b, h], ACT.Exp, scale=-1.0, bias=negmax1[:, b, h:h + 1],
                                            accum_out=den1[:, b, h:h + 1])

            act.wait_ge(w2_in, 16 * 2)
            nc.scalar.copy(w2_hi[:, :, 0:DO], w2[:, :, 0:DO]).then_inc(w2_hi_ready, 1)
            run_steps(act, step)

        @block.vector
        def _(dve):
            done = [0]

            def settle(last):
                done[0] += 1
                last.then_inc(setup_step, 1)
                dve.wait_ge(setup_step, done[0])

            def high_x(i, k):
                t = BODY * i + k
                dve.wait_ge(xT_in[k // PAIR % (RING // PAIR)], 16 * (BODY // RING * i + k // RING + 1))
                if begun(t, 2):
                    dve.wait_ge(xl_made, t - 1)
                nc.vector.tensor_copy(xT_hi[:, k % 2], xT_sb[:, k % RING]).then_inc(x_hi_done, 1)

            def layer2_scores(s):
                for h in range(H):
                    nc.vector.tensor_tensor_reduce(prod2[:, s, h], w2[:, h, 0:DO], att2_all[:, s], 1.0, 0.0, ALU.mult, ALU.add,
                                                   w2[:, h, DO + s:DO + s + 1]).then_inc(w2_scores_ready, 1)

            def layer2_bias():
                dve.wait_ge(colsum_made, 1)
                nc.vector.tensor_tensor(bias2[:, 0:DO], att2_all[:, 2], ps_xl2[:, 0:DO], ALU.subtract).then_inc(bias2_ready, 1)
                nc.vector.tensor_scalar(bias2[:, DO:W2C], ps_xl2[:, DO:W2C], -1.0, None, ALU.mult).then_inc(bias2_ready, 1)
                dve.wait_ge(bias2_ready, 2)

            def step(i, k):
                t = BODY * i + k
                if live(t, 0):
                    dve.wait_ge(xl_made, t + 1)
                    if begun(t, 4):
                        dve.wait_ge(u_made, t - 3)
                        dve.wait_ge(parts_done, t - 3)
                    if begun(t, 2):
                        dve.wait_ge(rows_made, t - 1)
                    score = ps_xl[:, :, HH * F:GW]
                    nc.vector.tensor_copy(parts[:, k % 2, 0:2, 0:H].rearrange("p s (j h) -> p j s h", j=HG),
                                          score.rearrange("p j (s h) -> p j s h", s=2))
                    nc.vector.tensor_copy(xl[:, k % 4, :, HH * F:GW], score).then_inc(scores_done, 1)
                    nc.vector.tensor_tensor(xl[:, k % 4, :, 0:HH * F], ps_xl[:, :, 0:HH * F], bias1[:], ALU.add).then_inc(xl_done, 1)
                if live(t, -1):
                    high_x(i, k + 1)
                if live(t, 6):
                    b, slot = (k - 6) % 2, (k - 6) % 4
                    dve.wait_ge(rstd_done, t - 5)
                    if begun(t, 10):
                        dve.wait_ge(y_out[slot // PAIR], 16 * (BODY // 4 * i + (k - 6) // 4))
                    nc.vector.tensor_scalar(y_sb[:, slot, :], resid[:, b, :], meanvar[:, b, 0:1], rstd[:, b:b + 1],
                                            ALU.subtract, ALU.mult).then_inc(y_done, 1)
                if live(t, -1):
                    make_mask(i, k + 1)
                if live(t, 1):
                    b = (k - 1) % 2
                    dve.wait_ge(prob1_done, t)
                    if begun(t, 3):
                        dve.wait_ge(attn1_done, t - 2)
                    nc.vector.reciprocal(rden1[:, b], den1[:, b]).then_inc(rden1_done, 1)
                if live(t, 0):
                    b = k % 2
                    dve.wait_ge(rows_done, 2 * t + 1)
                    if begun(t, 2):
                        dve.wait_ge(z1_made, t - 1)
                    nc.vector.tensor_tensor(pair_right[0:Q, b], src_rows[:, b].unsqueeze(1).broadcast_to([Q, H, P]), src_of[:],
                                            ALU.mult).then_inc(src_pairs_done, 1)
                if t_is(t, 0):
                    layer2_scores(1)
                if live(t, 5):
                    b = (k - 5) % 2
                    dve.wait_ge(resid_done, t - 4)
                    nc.vector.bn_stats(stats[:, b], resid[:, b]).then_inc(stats_done, 1)
                if t_is(t, 1):
                    layer2_bias()
                if live(t, 2):
                    b = (k - 2) % 2
                    dve.wait_ge(expu_done, t - 1)
                    if begun(t, 4):
                        dve.wait_ge(h_lo_done, t - 3)
                    nc.vector.scalar_tensor_tensor(hT[:, b], expu[:, b], 1.0, ps_u[:, :, :], ALU.min, ALU.max).then_inc(hT_done, 1)
                if live(t, 5):
                    dve.wait_ge(stats_done, t - 4)
                if live(t, 3):
                    b = (k - 3) % 2
                    dve.wait_ge(xl2_made, t - 2)
                    if begun(t, 5):
                        dve.wait_ge(u2_made, t - 4)
                    nc.vector.tensor_tensor(xl2[:, b], ps_xl2[:, 0:W2C], bias2[:], ALU.add).then_inc(xl2_done, 1)
                if live(t, 5):
                    b = (k - 5) % 2
                    nc.vector.bn_aggr(meanvar[:, b], stats[:, b]).then_inc(meanvar_done, 1)
                if live(t, 0):
                    dve.wait_ge(pos1_done, t + 1)
                    if begun(t, 2):
                        dve.wait_ge(prob1_done, t - 1)
                if live(t, 4):
                    b = (k - 4) % 2
                    dve.wait_ge(prob2_done, t - 3)
                    nc.vector.reciprocal(rden2[:, b:b + 1], den2[:, b:b + 1]).then_inc(rden2_done, 1)
                if live(t, 0):
                    b = k % 2
                    for h in range(H):
                        last = nc.vector.tensor_tensor_reduce(neg_lrelu1[:, b, h], ps_z1[:, h, :], pos1[:, b, h], -NEG_SLOPE, 3e38, ALU.add,
                                                              ALU.min, negmax1[:, b, h:h + 1])
                    last.then_inc(max1_done, 1)
                if live(t, 3):
                    b = (k - 3) % 2
                    dve.wait_ge(score2_done, t - 2)
                    if begun(t, 5):
                        dve.wait_ge(prob2_done, t - 4)
                    nc.vector.scalar_tensor_tensor(lrelu2[:, b], score2[:, b], NEG_SLOPE, score2[:, b], ALU.mult,
                                                   ALU.max).then_inc(lrelu2_done, 1)
                    dve.wait_ge(lrelu2_done, t - 2)
                    nc.vector.tensor_reduce(negmax2[:, b:b + 1], lrelu2[:, b], AX.X, ALU.max, negate=True).then_inc(max2_done, 1)
                if live(t, 4):
                    b = (k - 4) % 2
                    dve.wait_ge(x_in[(k - 4) // PAIR % (RING // PAIR)], 16 * (BODY // RING * i + (k - 4) // RING + 1))
                    dve.wait_ge(rden2_done, t - 3)
                    dve.wait_ge(u2_made, t - 3)
                    if begun(t, 6):
                        dve.wait_ge(y_done, t - 5)
                    nc.vector.scalar_tensor_tensor(resid[:, b], ps_u2, rden2[:, b:b + 1], x_sb[:, (k - 4) % RING],
                                                   ALU.mult, ALU.add).then_inc(resid_done, 1)

            def make_mask(i, k):
                t = BODY * i + k
                slot = k % RING
                dve.wait_ge(adj_in[slot // PAIR], 16 * (BODY // RING * i + k // RING + 1))
                if begun(t, RING):
                    dve.wait_ge(z2_made, t + 1 - RING)
                nc.vector.tensor_tensor(no_edge[:, slot], adj_sb[:, slot], edge_limit[:], ALU.is_le).then_inc(mask_done, 1)

            def low_w1(c, groups):
                return nc.vector.tensor_tensor(w1_lo[:, c, groups, 0:HH * F], w1[:, c, groups],
                                               w1_hi[:, c, groups, 0:HH * F].bitcast(F32), ALU.subtract)

            dve.wait_ge(consts_ready, 9)
            nc.vector.tensor_copy(ident_bf[:], ident[:])
            nc.vector.tensor_copy(ones_r[:], ones[:])
            for s in range(2):
                settle(nc.vector.tensor_reduce(part_of[s * Q:(s + 1) * Q], ident[s * Q:(s + 1) * Q, s * Q:s * Q + SPLIT * H]
                                               .rearrange("r (p h) -> r h p", h=H), AX.X, ALU.add))
            nc.vector.tensor_copy(src_of[:], part_of[0:Q].unsqueeze(2).broadcast_to([Q, H, P]))
            settle(nc.vector.tensor_reduce(any_part[:], part_of[0:Q], AX.X, ALU.add))
            for b in range(2):
                nc.vector.tensor_copy(pair_left[0:Q, b], any_part[:].broadcast_to([Q, P]))
                nc.vector.tensor_copy(pair_right[Q:2 * Q, b], part_of[Q:2 * Q].unsqueeze(2).broadcast_to([Q, H, P]))
            high_x(0, 0)
            dve.wait_ge(w1_in, 16)
            for c in reversed(range(KC)):
                nc.vector.tensor_copy(w1_hi[:, c, :, 0:HH * F], w1[:, c]).then_inc(w1_hi_ready, 1)
            dve.wait_ge(w1_hi_ready, KC)
            low_w1(KC - 1, slice(0, HG - 1))
            dve.wait_ge(w1_scores_made, 1)
            nc.vector.tensor_copy(w1_hi[:, :, :, HH * F:GW], ps_w1_scores).then_inc(w1_hi_ready, 1)
            for c in range(KC - 1):
                last = low_w1(c, slice(0, HG))
            last.then_inc(w1_ready, 1)
            dve.wait_ge(w1_hi_ready, KC + 1)
            nc.vector.tensor_tensor(w1_lo[:, :, :, HH * F:GW], ps_w1_scores, w1_hi[:, :, :, HH * F:GW].bitcast(F32),
                                    ALU.subtract).then_inc(w1_ready, 1)
            dve.wait_ge(b1_in, 16)
            settle(nc.vector.tensor_scalar(bias1[:], b1_all[:], 1.0, None, ALU.add))
            make_mask(0, 0)
            dve.wait_ge(w2_in, 16 * 2)
            layer2_scores(0)
            run_steps(dve, step)

        @block.tensor
        def _(pe):
            def step(i, k):
                t = BODY * i + k
                if live(t, 0):
                    pe.wait_ge(x_hi_done, t + 1)
                    if begun(t, 1):
                        pe.wait_ge(xl_done, t)
                    if t_is(t, 0):
                        pe.wait_ge(w1_hi_ready, KC + 1)
                    product1(xT_hi[:, k % 2], w1_hi, first=True)
                    pe.wait_ge(x_lo_done, t + 1)
                    product1(xT_lo[:, k % 2], w1_hi)
                    if t_is(t, 0):
                        pe.wait_ge(w1_ready, 3)
                    product1(xT_hi[:, k % 2], w1_lo, final=True).then_inc(xl_made, 1)
                if t_is(t, 1):
                    layer2_column_sums()
                if live(t, 2):
                    b = (k - 2) % 2
                    pe.wait_ge(attn1T_done, t - 1)
                    if begun(t, 3):
                        pe.wait_ge(hT_done, t - 2)
                    for h in range(H):
                        j, hh = h // HH, h % HH
                        last = nc.tensor.matmul(ps_u[:, h, :], xl[:, (k - 2) % 4, j, hh * F:(hh + 1) * F], attn1T[:, b, h],
                                                start=True, stop=True)
                    last.then_inc(u_made, 1)
                if t_is(t, 3):
                    pe.wait_ge(bias2_ready, 2)
                if live(t, 3):
                    pe.wait_ge(h_hi_done, t - 2)
                    if begun(t, 4):
                        pe.wait_ge(xl2_done, t - 3)
                    product2((k - 3) % 2, 0, EARLY)
                if live(t, 4):
                    b = (k - 4) % 2
                    pe.wait_ge(prob2_done, t - 3)
                    if begun(t, 5):
                        pe.wait_ge(resid_done, t - 4)
                    nc.tensor.transpose(ps_p2T, prob2[:, b], ident[:]).then_inc(p2T_made, 1)
                if live(t, 0):
                    pe.wait_ge(parts_done, t + 1)
                    if begun(t, 4):
                        pe.wait_ge(score2_done, t - 3)
                    nc.tensor.transpose(ps_rows, parts[:, k % 2].rearrange("p s c -> p (s c)"), ident_bf[:]).then_inc(rows_made, 1)
                if live(t, 3):
                    product2((k - 3) % 2, EARLY, 2 * H)
                    pe.wait_ge(h_lo_done, t - 2)
                    product2((k - 3) % 2, 2 * H, 3 * H).then_inc(xl2_made, 1)
                if live(t, 0):
                    b = k % 2
                    if t_is(t, 0):
                        pe.wait_ge(mask_ident_ready, 1)
                    pe.wait_ge(mask_done, t + 1)
                    pe.wait_ge(rows_done, 2 * t + 2)
                    pe.wait_ge(src_pairs_done, t + 1)
                    if begun(t, 1):
                        pe.wait_ge(max1_done, t)
                    z = ps_z1[:].rearrange("p h d -> p (h d)")
                    nc.tensor.matmul(z, no_edge[:, k % RING], mask_ident[:].rearrange("p h d -> p (h d)"), start=True, stop=False)
                    nc.tensor.matmul(z, pair_left[:, b], pair_right[:, b].rearrange("p h d -> p (h d)"), start=False,
                                     stop=True).then_inc(z1_made, 1)
                if live(t, 4):
                    b = (k - 4) % 2
                    pe.wait_ge(prob2T_done, t - 3)
                    nc.tensor.matmul(ps_u2, prob2T[:, b], xl2[:, b, 0:DO], start=True, stop=True).then_inc(u2_made, 1)
                if live(t, 1):
                    b = (k - 1) % 2
                    pe.wait_ge(attn1_done, t)
                    if begun(t, 2):
                        pe.wait_ge(attn1T_done, t - 1)
                    for h in range(H):
                        last = nc.tensor.transpose(ps_pT[:, h, :], attn1[:, b, h], ident[:])
                    last.then_inc(pT_made, 1)
                if live(t, 3):
                    b = (k - 3) % 2
                    pe.wait_ge(xl2_done, t - 2)
                    if begun(t, 3) and live(t, 0):
                        pe.wait_ge(rows_done, 2 * t + 2)
                    if begun(t, 4):
                        pe.wait_ge(score2_done, t - 3)
                    nc.tensor.matmul(ps_z2, no_edge[:, (k - 3) % RING], mask_ident[:, 0, :], start=True, stop=False)
                    nc.tensor.matmul(ps_z2, xl2[:, b, DO:DO + 1].broadcast_to([P, P]), ident[:],
                                     start=False, stop=True).then_inc(z2_made, 1)

            def product1(x_part, w_part, first=False, final=False):
                for j in range(HG):
                    for c in range(KC):
                        last = nc.tensor.matmul(ps_xl[:, j, 0:GW], x_part[:, c, :], w_part[:, c, j, :],
                                                start=(first and c == 0), stop=(final and c == KC - 1))
                return last

            def product2(b, begin, end):
                for m in range(begin, end):
                    h_part = hT_hi if m < 2 * H else hT_lo
                    w_part = w2_lo if H <= m < 2 * H else w2_hi
                    last = nc.tensor.matmul(ps_xl2[:, 0:W2C], h_part[:, b, m % H], w_part[:, m % H, :], start=(m == 0),
                                            stop=(m == 3 * H - 1))
                return last

            def layer2_column_sums():
                pe.wait_ge(w2_ready, 2)
                for h in range(H):
                    nc.tensor.matmul(ps_xl2[:, 0:W2C], ones_r[:], w2_hi[:, h, :], start=(h == 0), stop=False)
                    last = nc.tensor.matmul(ps_xl2[:, 0:W2C], ones_r[:], w2_lo[:, h, :], start=False, stop=(h == H - 1))
                last.then_inc(colsum_made, 1)

            pe.wait_ge(consts_ready, 9)
            pe.wait_ge(w1T_in, 16 * 2)
            by_head = ps_w1_scores.rearrange("p c j (s h) -> p c j h s", s=2)
            for c in range(KC):
                for h in range(H):
                    last = nc.tensor.matmul(by_head[:, c, h // HH, h % HH, :], w1T[:, h, c, :], att1[:, h, :], start=True, stop=True)
            last.then_inc(w1_scores_made, 1)
            run_steps(pe, step)


def t_is(t, number):
    return isinstance(t, int) and t == number


def kernel(**inputs):
    import numpy as _np
    import concourse.bacc as _bacc
    from concourse import mybir as _mybir
    from concourse.bass_utils import run_bass_kernel_spmd as _run

    nc = _bacc.Bacc("TRN2", target_bir_lowering=False, num_devices=1)
    x, adj = _np.asarray(inputs['x']), _np.asarray(inputs['adj'])
    B, N, D = x.shape
    laid = {
        'x': x.reshape(B // 2, 2, N, D).transpose(0, 2, 1, 3),
        'xT': x.reshape(B // 2, 2, N, D // P, P).transpose(0, 4, 1, 3, 2).reshape(B // 2, P, 2, -1),
        'adj': adj.reshape(B // 2, 2, N, N).transpose(0, 2, 1, 3),
    }
    W1, W2 = _np.asarray(inputs['L0_gnn_W1']), _np.asarray(inputs['L0_gnn_W2'])
    H = inputs['L0_gnn_att_src1'].shape[0]
    columns = lambda names: _np.stack([_np.asarray(inputs[n]) for n in names], axis=-1)
    laid['W1'] = W1
    laid['W1T'] = W1.reshape(D, H, P).transpose(2, 1, 0).reshape(P, -1)
    laid['att1'] = columns(['L0_gnn_att_src1', 'L0_gnn_att_dst1']).transpose(1, 0, 2)
    laid['b1'] = inputs['L0_gnn_b1']
    laid['W2'] = W2
    laid['att2_b2'] = _np.concatenate([_np.asarray(inputs[n]).reshape(-1) for n in
                                       ('L0_gnn_att_src2', 'L0_gnn_att_dst2', 'L0_gnn_b2')])
    arrays, args = {}, []
    for name, a in laid.items():
        a = _np.ascontiguousarray(a)
        arrays[f"in_{name}_dram"] = a
        args.append(nc.dram_tensor(f"in_{name}_dram", a.shape, _mybir.dt.from_np(a.dtype), kind="ExternalInput").ap())
    args.append(nc.dram_tensor("out_0_dram", (B // 2, N, 2, D), _mybir.dt.float32, kind="ExternalOutput").ap())
    gat_block_program(nc, *args)
    r = _run(nc, [arrays], core_ids=[0])
    return r.results[0]["out_0_dram"].transpose(0, 2, 1, 3).reshape(B, N, D)
```
